# Optimizing a Trainium2 kernel written in Bass

```python
import numpy as np
import jax
import jax.numpy as jnp

def _softmax(x, axis=-1):
    return jax.nn.softmax(x, axis=axis)

def _gelu(x):
    return jax.nn.gelu(x, approximate=True)

def _silu(x):
    return jax.nn.silu(x)

def _sigmoid(x):
    return jax.nn.sigmoid(x)

def _layernorm(x, axis=-1, eps=1e-05):
    m = jnp.mean(x, axis=axis, keepdims=True)
    v = jnp.var(x, axis=axis, keepdims=True)
    return (x - m) / jnp.sqrt(v + eps)

def _scatter_add(tgt, idx, src, axis=0):
    return tgt.at[idx].add(src)

def _segment_sum(src, seg, n):
    return jax.ops.segment_sum(src, seg, n)
kernel_name = 'mk_gnn_resnorm_d2_gnn_r8_06acff'

def setup_inputs(seed: int=0):
    np.random.seed(seed)
    _w = jnp.asarray

    def _rec_inputs():
        import jax
        import jax.numpy as jnp
        _gk = jax.random.key(seed)
        x = -0.0005121 + 1.001 * jax.random.normal(jax.random.fold_in(_gk, 1), (12500, 32), jnp.float32)
        src = jax.random.randint(jax.random.fold_in(_gk, 2), (200000,), 0, 12500, jnp.int32)
        dst = jnp.minimum((12500 * jax.random.uniform(jax.random.fold_in(_gk, 3), (200000,)) ** 2.0).astype(jnp.int32), 99999)
        _o = jnp.argsort(dst, stable=True)
        src = src[_o]
        dst = dst[_o]
        edge_attr_4 = 0.00109026 + 0.999989 * jax.random.normal(jax.random.fold_in(_gk, 12), (200000, 4), jnp.float32)
        edge_attr_8 = jax.random.uniform(jax.random.fold_in(_gk, 13), (200000, 8), jnp.float32, 0.0, 1)
        edge_weight = jax.random.uniform(jax.random.fold_in(_gk, 14), (200000,), jnp.float32, 0.0, 1)
        return (x, src, dst, edge_attr_4, edge_attr_8, edge_weight)
    x, src, dst, edge_attr_4, edge_attr_8, edge_weight = _rec_inputs()

    def _L0_gnn_setup():
        import jax, jax.numpy as jnp
        import numpy as np
        N_NODES = 12500
        N_EDGES = 200000
        D_FEAT = 32
        key = jax.random.key(seed)
        k1, k2, k3, k4 = jax.random.split(key, 4)
        features = jax.random.normal(k1, (N_NODES, D_FEAT), dtype=jnp.float32)
        row = jax.random.randint(k2, (N_EDGES,), 0, N_NODES, dtype=jnp.int32)
        col = jax.random.randint(k3, (N_EDGES,), 0, N_NODES, dtype=jnp.int32)
        edge_weight = jax.random.uniform(k4, (N_EDGES,), dtype=jnp.float32)
        return {'features': features, 'row': row, 'col': col, 'edge_weight': edge_weight}
    _L0_gnn_all = _L0_gnn_setup()
    _L0_gnn_in = {k: v for k, v in _L0_gnn_all.items() if k in ()}
    del _L0_gnn_all

    def _L1_gnn_setup():
        import jax, jax.numpy as jnp
        import numpy as np
        MUL = 8
        INV_SQRT3 = float(1.0 / np.sqrt(3.0))
        A_SCALAR = float(np.sqrt(1.0 / 128.0))
        A_VECTOR = float(np.sqrt(3.0 / 128.0))
        SQRT2 = float(np.sqrt(2.0))
        N_NODES, N_EDGES, NUM_BASIS, HIDDEN = (6250, 100000, 8, 256)
        WEIGHT_NUMEL = 4 * MUL * MUL
        k = jax.random.split(jax.random.key(seed), 7)
        node_features = jax.random.normal(k[0], (N_NODES, 4 * MUL), jnp.float32)
        edge_src = jax.random.randint(k[1], (N_EDGES,), 0, N_NODES)
        edge_dst = jax.random.randint(k[2], (N_EDGES,), 0, N_NODES)
        edge_sh = jax.random.normal(k[3], (N_EDGES, 4), jnp.float32)
        edge_scalars = jax.random.uniform(k[4], (N_EDGES, NUM_BASIS), jnp.float32)
        fc_w1 = jax.random.normal(k[5], (NUM_BASIS, HIDDEN), jnp.float32)
        fc_w2 = jax.random.normal(k[6], (HIDDEN, WEIGHT_NUMEL), jnp.float32)
        return dict(node_features=node_features, edge_src=edge_src, edge_dst=edge_dst, edge_sh=edge_sh, edge_scalars=edge_scalars, fc_w1=fc_w1, fc_w2=fc_w2)
    _L1_gnn_all = _L1_gnn_setup()
    _L1_gnn_in = {k: v for k, v in _L1_gnn_all.items() if k in ('fc_w1', 'fc_w2')}
    del _L1_gnn_all
    return {'x': x, 'src': src, 'dst': dst, 'edge_attr_4': edge_attr_4, 'edge_attr_8': edge_attr_8, 'edge_weight': edge_weight, 'L1_gnn_fc_w1': _L1_gnn_in['fc_w1'], 'L1_gnn_fc_w2': _L1_gnn_in['fc_w2']}

def reference(x, src, dst, edge_attr_4, edge_attr_8, edge_weight, L1_gnn_fc_w1, L1_gnn_fc_w2):
    import jax
    import jax.numpy as jnp

    def _L0_gnn_ref(features, row, col, edge_weight):
        import jax, jax.numpy as jnp
        import numpy as np
        N_NODES = 12500
        N_EDGES = 200000
        D_FEAT = 32
        gathered = features[col] * edge_weight[:, None]
        out = jax.ops.segment_sum(gathered, row, num_segments=N_NODES)
        return out

    def _L1_gnn_ref(node_features, edge_src, edge_dst, edge_sh, edge_scalars, fc_w1, fc_w2):
        import jax, jax.numpy as jnp
        import numpy as np
        MUL = 8
        INV_SQRT3 = float(1.0 / np.sqrt(3.0))
        A_SCALAR = float(np.sqrt(1.0 / 128.0))
        A_VECTOR = float(np.sqrt(3.0 / 128.0))
        SQRT2 = float(np.sqrt(2.0))
        N_NODES, N_EDGES, NUM_BASIS, HIDDEN = (6250, 100000, 8, 256)
        WEIGHT_NUMEL = 4 * MUL * MUL
        N = node_features.shape[0]
        E = edge_src.shape[0]
        h = jax.nn.relu(edge_scalars @ (fc_w1 * (1.0 / np.sqrt(NUM_BASIS)))) * SQRT2
        w = (h @ (fc_w2 * (1.0 / np.sqrt(HIDDEN)))).reshape(E, 4, MUL, MUL)
        x = node_features[edge_src]
        s1 = x[:, :MUL]
        v1 = x[:, MUL:].reshape(E, MUL, 3)
        s2 = edge_sh[:, 0]
        v2 = edge_sh[:, 1:4]
        out_s = A_SCALAR * (jnp.einsum('eu,euw->ew', s1 * s2[:, None], w[:, 0]) + INV_SQRT3 * jnp.einsum('eui,ei,euw->ew', v1, v2, w[:, 1]))
        out_v = A_VECTOR * INV_SQRT3 * (jnp.einsum('eu,euw,ei->ewi', s1, w[:, 2], v2) + jnp.einsum('eui,euw->ewi', v1 * s2[:, None, None], w[:, 3]))
        edge_features = jnp.concatenate([out_s, out_v.reshape(E, 3 * MUL)], axis=1)
        node_out = jax.ops.segment_sum(edge_features, edge_dst, num_segments=N)
        return node_out * (1.0 / np.sqrt(E / N))
    x = _layernorm(x + _L0_gnn_ref(x, src, dst, edge_weight), axis=-1)
    x = _layernorm(x + _L1_gnn_ref(x, src, dst, edge_attr_4, edge_attr_8, L1_gnn_fc_w1, L1_gnn_fc_w2), axis=-1)
    return x

_drawn_inputs = setup_inputs


def setup_inputs(seed=0):
    import zlib

    import numpy as np

    out = dict(_drawn_inputs(seed))
    spreads = {}
    factors = {}
    for name, (base, spread) in spreads.items():
        noise = np.random.default_rng([zlib.crc32(name.encode()), seed]).standard_normal(out[name].shape)
        drawn = base * np.exp(spread * noise) if base else spread * noise
        out[name] = jnp.asarray(drawn.astype(out[name].dtype))
    for name, factor in factors.items():
        out[name] = (out[name] * factor).astype(out[name].dtype)
    return out
```

```python
from contextlib import ExitStack

import concourse.bass as bass
from concourse import mybir

F32 = mybir.dt.float32
BF16 = mybir.dt.bfloat16
I32 = mybir.dt.int32
ALU = mybir.AluOpType
ACT = mybir.ActivationFunctionType
AX_X = mybir.AxisListType.X

P = 128
N, E, D = 12500, 200000, 32
MUL, BASIS, HID = 8, 8, 256
T = 4
SB = P * T
U = 8
TURNS = -(-E // (SB * U))
NSB = TURNS * U
EP = NSB * SB
NJ = -(-N // P)
NP = P * NJ
ROWS = NP + P
WIN = P
SLOTS = 4
PRIME = 6
EPS = 1e-5
ESCOLS = 8 * EP // P
ESPART = ESCOLS // 8
NSPLIT = 3
KROWS = NSPLIT * NSPLIT * BASIS
CHUNK = 4


def after(s):
    return s + (1 + PRIME)


def spread(ap, axis, count):
    ap = ap.unsqueeze(axis)
    shape = list(ap.shape)
    shape[axis] = count
    return ap.to_broadcast(shape)


def gnn_kernel(nc, x, src, dst, first, weight, sh, es, w1, w2, out):
    tables = [nc.dram_tensor(f"table{t}", [ROWS, D], F32, kind="Internal").ap() for t in range(T)]
    nodes1 = nc.dram_tensor("nodes1", [NP, D], F32, kind="Internal").ap()
    es_split = nc.dram_tensor("es_split", [NSPLIT * BASIS, EP], BF16, kind="Internal").ap()

    ctx = ExitStack()
    with ctx:
        def sb(name, shape, dt=F32):
            return ctx.enter_context(nc.sbuf_tensor(name, shape, dt))

        def sem(name):
            return ctx.enter_context(nc.semaphore(name))

        src_i = sb("src_i", [P, NSB * T], I32)
        dst_i = sb("dst_i", [P, NSB * T], I32)
        first_i = sb("first_i", [P, NSB], I32)
        rel = sb("rel", [P, NSB * T])
        wgt = sb("wgt", [P, NSB * T])
        sh_sb = sb("sh_sb", [P, NSB * T * 4])
        big = sb("big", [P, ROWS])
        x1 = sb("x1", [P, NJ * D])
        work = sb("work", [P, NJ * D])
        stat = sb("stat", [P, 4, NJ])
        iota_sb = sb("iota_sb", [P, P])
        tri = sb("tri", [P, P])
        ident = sb("ident", [P, P])
        identb = sb("identb", [P, P], BF16)
        onescol = sb("onescol", [P, 1])
        zeros = sb("zeros", [P, ROWS // P * D])
        trash = sb("trash", [P, 1])
        eps = sb("eps", [P, 1])
        ext = sb("ext", [P, 8])
        flag_i = sb("flag_i", [1, 1], I32)
        w1s = sb("w1s", [KROWS, 6, HID])
        w1p = sb("w1p", [KROWS, NSPLIT, HID], BF16)
        w1m = sb("w1m", [KROWS, NSPLIT])
        w1k = sb("w1k", [KROWS, HID], BF16)
        w2s = sb("w2s", [P, 2, HID])
        keyf = sb("keyf", [P, 2, T])
        oh_b = sb("oh_b", [P, 2, T, WIN], BF16)
        oht = sb("oht", [P, 2, T, P])
        oh = sb("oh", [P, 2, T, WIN])
        same = sb("same", [P, 2, T, P])
        junk = sb("junk", [P, T, P])
        dup = sb("dup", [P, 2, 3, T])
        xwin = sb("xwin", [P, SLOTS, D])
        msg = sb("msg", [P, 2, T, D])
        comb = sb("comb", [P, SLOTS, T, D])
        sidx = sb("sidx", [P, SLOTS, T], I32)
        gidx = sb("gidx", [P, SLOTS, T], I32)
        gat = sb("gat", [P, SLOTS, T, D])
        hs = sb("hs", [KROWS, 2, CHUNK * SB], BF16)
        hT = sb("hT", [P, 2, 2, SB])
        vv = sb("vv", [P, T, MUL, 3])
        vdot = sb("vdot", [P, T, MUL])
        prod_s = sb("prod_s", [P, T, MUL, 2 * MUL])
        prod_b = sb("prod_b", [P, T, MUL, MUL])
        prod_v = sb("prod_v", [P, 3, T, MUL, MUL])
        side = sb("side", [P, T, 4, MUL])

        ps_w = ctx.enter_context(nc.psum_tensor("ps_w", [P, 4, 512], F32))
        ps_h = ctx.enter_context(nc.psum_tensor("ps_h", [P, 2, 512], F32))
        ps_d = ctx.enter_context(nc.psum_tensor("ps_d", [P, 512], F32))
        ps_a = ctx.enter_context(nc.psum_tensor("ps_a", [P, 512], F32))
        es_f = big[:, 0:ESPART]
        es_r = big[:, ESPART:2 * ESPART]
        es_b = [big[:, (4 + m) * ESPART // 2:(5 + m) * ESPART // 2].bitcast(BF16) for m in range(NSPLIT)]
        iota_ps = ps_d[:, 0:P]
        red = ps_d[:, P:P + T * 6 * MUL].rearrange("p (t c w) -> p t c w", t=T, c=6)
        oht_ps = ps_w[:, 0, 0:SB // 2].bitcast(BF16).rearrange("p (t e) -> p t e", t=T)
        x_ps = ps_w[:, 1, 0:T * D].rearrange("p (t f) -> p t f", t=T)
        key_ps0 = ps_w[:, 2, :].rearrange("p (t e) -> p t e", t=T)
        comb_ps0 = ps_w[:, 3, 0:T * D].rearrange("p (t f) -> p t f", t=T)
        key_ps1 = ps_a[:, :].rearrange("p (t e) -> p t e", t=T)
        comb_ps1 = ps_a[:, 0:T * D].rearrange("p (t f) -> p t f", t=T)

        s_edges, s_w, s_sh, s_wload, s_init = map(sem, ("s_edges", "s_w", "s_sh", "s_wload", "s_init"))
        s_const, s_iotab, s_zero, s_step, s_flag, s_flagps = map(
            sem, ("s_const", "s_iotab", "s_zero", "s_step", "s_flag", "s_flagps"))
        s_w1k, s_w2, s_link, s_ext = sem("s_w1k"), sem("s_w2"), sem("s_link"), sem("s_ext")
        s_es, s_esa, s_esb, s_esr, s_esc, s_esout = map(
            sem, ("s_es", "s_esa", "s_esb", "s_esr", "s_esc", "s_esout"))
        s_tab = sem("s_tab")
        s_x1out, s_out = sem("s_x1out"), sem("s_out")
        s_turned, s_turned_read = sem("s_turned"), sem("s_turned_read")
        s_landed = [sem(f"s_landed{n}") for n in range(2)]
        s_centred = [sem(f"s_centred{n}") for n in range(2)]
        s_squared = [sem(f"s_squared{n}") for n in range(2)]
        s_summed = [sem(f"s_summed{n}") for n in range(2)]
        s_std = [sem(f"s_std{n}") for n in range(2)]
        s_normed = [sem(f"s_normed{n}") for n in range(2)]

        def layer_sems(n):
            return {name: sem(f"{name}{n}") for name in (
                "keyf", "oh", "oht_ps", "oht", "key_ps", "same", "key_free", "sidx", "x_ps",
                "msg", "comb_ps", "comb", "retired", "gidx", "hps0", "hps1", "ht0", "ht1",
                "w_ps", "w_free", "pre", "dot", "ps", "pv", "pb", "rs", "rv", "rb", "scaled",
                "cross", "outer", "asked", "acc", "added")}
        L = [layer_sems(0), layer_sems(1)]
        s_xwin = [sem(f"s_xwin{q}") for q in range(SLOTS)]
        s_gat = [[sem(f"s_gat{n}_{q}") for q in range(SLOTS)] for n in range(2)]
        s_scat = [[sem(f"s_scat{n}_{t}") for t in range(T)] for n in range(2)]
        s_hs = [sem(f"s_hs{b}") for b in range(2)]

        block = ctx.enter_context(nc.Block())

        def sweep(eng, step, head=0):
            for i in range(head):
                for k in range(U):
                    step(i * U + k, k, i, lambda d: True)
            with eng.Fori(head, TURNS - 1) as i:
                for k in range(U):
                    step(i * U + k, k, i, lambda d: True)
            for k in range(U):
                step((TURNS - 1) * U + k, k, TURNS - 1, lambda d: k + d < U)

        def uses(i, k):
            return i * (U // SLOTS) + k // SLOTS

        def both(eng, program):
            eng.wait_ge(s_flag, 1)
            flag = eng.value_load(flag_i[0:1, 0:1], min_val=0, max_val=1)
            with eng.If(flag == 0):
                program(True)
            with eng.Else():
                program(False)

        @block.sync
        def _(eng):
            eng.dma_start(dst_i[:, :], dst).then_inc(s_edges, 16)
            eng.dma_start(first_i[:, :], first).then_inc(s_edges, 16)
            eng.dma_start(src_i[:, :], src).then_inc(s_edges, 16)
            eng.dma_start(wgt[:, :], weight).then_inc(s_w, 16)
            for q in range(NSPLIT * NSPLIT):
                eng.dma_start(w1s[q * BASIS:(q + 1) * BASIS, 0, :], w1).then_inc(s_wload, 16)
            eng.dma_start(w2s[:, :, :], w2.rearrange("(c p) n -> p c n", c=2)).then_inc(s_wload, 16)
            eng.dma_start(sh_sb[:, :], sh).then_inc(s_sh, 16)
            eng.dma_start(tables[0].rearrange("(p r) f -> p (r f)", p=P),
                          x.rearrange("(p r) f -> p (r f)", p=P)).then_inc(s_init, 16)
            eng.wait_ge(s_zero, 1)
            for t in range(1, T):
                eng.dma_start(tables[t].rearrange("(p r) f -> p (r f)", p=P), zeros[:, :]).then_inc(s_init, 16)
            es_out = es_split.rearrange("(m r) (c n) -> m (r c) n", m=NSPLIT, c=P // BASIS)
            es_in = es.rearrange("r (c n) -> (r c) n", c=P // BASIS)
            for q in range(8):
                if q:
                    eng.wait_ge(s_esout, 48 * q)
                eng.dma_start(es_f, es_in[:, q * ESPART:(q + 1) * ESPART]).then_inc(s_es, 16)
                eng.wait_ge(s_esc, q + 1)
                for m in range(NSPLIT):
                    eng.dma_start(es_out[m, :, q * ESPART:(q + 1) * ESPART], es_b[m]).then_inc(s_esout, 16)

            def load_tables():
                for t in range(T):
                    eng.dma_start(big[:, t * NJ * D:(t + 1) * NJ * D],
                                  tables[t][0:NP, :].rearrange("(p r) f -> p (r f)", p=P)).then_inc(s_tab, 16)

            def program(fast):
                if fast:
                    def window(s, k, i, more):
                        base = eng.value_load(first_i[0:1, bass.ds(s, 1)], min_val=0, max_val=N - 1)
                        eng.wait_ge(L[0]["x_ps"], after(s - SLOTS))
                        eng.dma_start(xwin[:, k % SLOTS, :], x[bass.ds(base, WIN), :]).then_inc(s_xwin[k % SLOTS], 16)
                    eng.wait_ge(s_edges, 48)
                    sweep(eng, window)
                eng.wait_ge(s_esout, 48 * 8)
                eng.wait_ge(s_landed[0], 1)
                load_tables()
                eng.wait_ge(s_normed[0], 1)
                eng.dma_start(nodes1.rearrange("(p r) f -> p (r f)", p=P), x1[:, :]).then_inc(s_x1out, 16)
                if not fast:
                    eng.wait_ge(s_tab, 16 * T)
                    for t in range(T):
                        eng.dma_start(tables[t].rearrange("(p r) f -> p (r f)", p=P), zeros[:, :]).then_inc(s_init, 16)

                def scalars(s, k, i, more):
                    if k % CHUNK:
                        return
                    eng.wait_ge(L[1]["hps1"], after(s - CHUNK - 1))
                    b = k // CHUNK
                    for m in range(NSPLIT):
                        eng.dma_start(hs[m * NSPLIT * BASIS:(m + 1) * NSPLIT * BASIS, b, :],
                                      es_split[:, bass.ds(s * SB, CHUNK * SB)]).then_inc(s_hs[b], 16)
                sweep(eng, scalars)
                if not fast:
                    eng.wait_ge(s_landed[1], 1)
                    load_tables()
                eng.wait_ge(s_normed[1], 1)
                eng.dma_start(out.rearrange("(p r) f -> p (r f)", p=P), work[:, :]).then_inc(s_out, 16)
                eng.wait_ge(s_x1out, 16)
                eng.wait_ge(s_out, 16)
            both(eng, program)

        @block.gpsimd
        def _(eng):
            nc.gpsimd.memset(zeros[:, :], 0.0).then_inc(s_zero, 1)
            nc.gpsimd.iota(iota_sb[:, :], pattern=[[1, P]], base=0, channel_multiplier=0,
                           allow_small_or_imprecise_dtypes=True).then_inc(s_const, 1)
            nc.gpsimd.iota(trash[:, :], pattern=[[0, 1]], base=NP, channel_multiplier=1,
                           allow_small_or_imprecise_dtypes=True).then_inc(s_const, 1)
            nc.gpsimd.memset(eps[:, :], EPS).then_inc(s_const, 1)
            nc.gpsimd.memset(onescol[:, :], 1.0).then_inc(s_const, 1)
            nc.gpsimd.memset(tri[:, :], 1.0).then_inc(s_const, 1)
            nc.gpsimd.memset(ident[:, :], 0.0).then_inc(s_const, 1)
            nc.gpsimd.memset(identb[:, :], 0.0).then_inc(s_const, 1)
            nc.gpsimd.memset(w1m[:, :], 1.0).then_inc(s_const, 1)
            eng.wait_ge(s_const, 8)
            nc.gpsimd.affine_select(out=tri[:, :], in_=tri[:, :], compare_op=ALU.is_gt, fill=0.0,
                                    base=0, pattern=[[-1, P]], channel_multiplier=1).then_inc(s_const, 1)
            for m in (ident, identb):
                nc.gpsimd.affine_select(out=m[:, :], in_=m[:, :], compare_op=ALU.not_equal, fill=1.0,
                                        base=0, pattern=[[-1, P]], channel_multiplier=1).then_inc(s_const, 1)
            nc.gpsimd.affine_select(out=w1m[:, :], in_=w1m[:, :], compare_op=ALU.is_ge, fill=0.0,
                                    base=0, pattern=[[-NSPLIT * BASIS, NSPLIT]],
                                    channel_multiplier=1).then_inc(s_const, 1)
            eng.wait_ge(s_const, 12)
            nc.gpsimd.affine_select(out=w1m[:, :], in_=w1m[:, :], compare_op=ALU.is_ge, fill=0.0,
                                    base=NSPLIT * BASIS - 1, pattern=[[NSPLIT * BASIS, NSPLIT]],
                                    channel_multiplier=-1).then_inc(s_const, 1)

            def gather(n, s, k, i, table):
                q = k % SLOTS
                eng.wait_ge(L[n]["gidx"], after(s))
                eng.wait_ge(L[n]["msg" if n == 0 else "pv"], after(s - SLOTS))
                eng.sem_inc(L[n]["asked"], 1)
                for t in range(T):
                    nc.gpsimd.indirect_dma_start(
                        out=gat[:, q, t, :], out_offset=None, in_=table,
                        in_offset=bass.IndirectOffsetOnAxis(ap=gidx[:, q, t:t + 1], axis=0),
                    ).then_inc(s_gat[n][q], 16)

            def first_one(s):
                return isinstance(s, int) and s == 0

            def scatter(n, s, k, head):
                q = k % SLOTS
                eng.wait_ge(L[n]["comb"], after(s))
                eng.wait_ge(L[n]["sidx"], after(s))
                for t in range(T):
                    if head:
                        eng.wait_ge(s_init, 16 * T * (n + 1))
                    else:
                        eng.wait_ge(s_scat[n][t], s * 16)
                    eng.sem_inc(L[n]["retired"], 1)
                    nc.gpsimd.indirect_dma_start(
                        out=tables[t], out_offset=bass.IndirectOffsetOnAxis(ap=sidx[:, q, t:t + 1], axis=0),
                        in_=comb[:, q, t, :], in_offset=None, compute_op=ALU.add,
                    ).then_inc(s_scat[n][t], 16)

            def program(fast):
                eng.sem_inc(L[0]["retired"], 3 * T)
                if fast:
                    sweep(eng, lambda s, k, i, more: scatter(0, s, k, first_one(s)), head=1)
                else:
                    for k in range(2):
                        gather(0, k, k, 0, x)

                    def step(s, k, i, more):
                        if more(2):
                            gather(0, s + 2, k + 2, i, x)
                        scatter(0, s, k, first_one(s))
                    sweep(eng, step, head=1)
                for t in range(T):
                    eng.wait_ge(s_scat[0][t], NSB * 16)
                eng.sem_inc(s_landed[0], 1)
                eng.wait_ge(s_x1out, 16)
                if fast:
                    sweep(eng, lambda s, k, i, more: gather(1, s, k, i, nodes1))
                else:
                    eng.sem_inc(L[1]["retired"], 3 * T)
                    for k in range(2):
                        gather(1, k, k, 0, nodes1)

                    def step(s, k, i, more):
                        if more(2):
                            gather(1, s + 2, k + 2, i, nodes1)
                        scatter(1, s, k, first_one(s))
                    sweep(eng, step, head=1)
                    for t in range(T):
                        eng.wait_ge(s_scat[1][t], NSB * 16)
                    eng.sem_inc(s_landed[1], 1)
            both(eng, program)

        @block.scalar
        def _(eng):
            eng.wait_ge(s_const, 13)
            nc.scalar.activation(iota_ps, iota_sb[:, :], ACT.Copy).then_inc(s_iotab, 1)
            for q in range(8):
                eng.wait_ge(s_es, 16 * (q + 1))
                nc.scalar.activation(es_b[0], es_f, ACT.Copy).then_inc(s_esa, 1)
                eng.wait_ge(s_esr, q + 1)
                nc.scalar.activation(es_b[1], es_r, ACT.Copy).then_inc(s_esb, 1)

            def index(n, s, k, i, ids):
                eng.wait_ge(L[n]["msg" if n == 0 else "pv"], after(s - SLOTS))
                nc.scalar.activation(gidx[:, k % SLOTS, :], ids[:, bass.ds(s * T, T)], ACT.Copy)\
                    .then_inc(L[n]["gidx"], 1)

            def one_hot_out(s, k):
                eng.wait_ge(L[0]["oht_ps"], after(s))
                nc.scalar.activation(oht[:, k % 2, :, :], oht_ps, ACT.Copy).then_inc(L[0]["oht"], 1)

            def comb_out(n, s, k):
                eng.wait_ge(L[n]["comb_ps"], after(s))
                eng.wait_ge(L[n]["retired"], s * T + T)
                nc.scalar.activation(comb[:, k % SLOTS, :, :], comb_ps0 if n == 0 else comb_ps1, ACT.Copy)\
                    .then_inc(L[n]["comb"], 1)

            def hidden(s, k):
                for c in range(2):
                    eng.wait_ge(L[1][f"hps{c}"], after(s))
                    nc.scalar.activation(hT[:, k % 2, c, :], ps_h[:, c, :], ACT.Relu,
                                         scale=(2.0 / BASIS) ** 0.5).then_inc(L[1][f"ht{c}"], 1)

            def norm(n):
                eng.wait_ge(s_centred[n], 1)
                nc.scalar.activation(big[:, 0:NJ * D], work[:, :], ACT.Square).then_inc(s_squared[n], 1)
                eng.wait_ge(s_summed[n], 1)
                nc.scalar.activation(stat[:, 2, :], stat[:, 1, :], ACT.Sqrt, bias=eps[:, :],
                                     scale=1.0 / D).then_inc(s_std[n], 1)

            def program(fast):
                eng.sem_inc(L[0]["comb"], PRIME)
                eng.sem_inc(L[0]["oht"], PRIME)
                eng.sem_inc(L[0]["gidx"], PRIME)
                eng.sem_inc(L[1]["gidx"], PRIME)
                eng.sem_inc(L[1]["comb"], PRIME)
                eng.sem_inc(L[1]["ht0"], PRIME)
                eng.sem_inc(L[1]["ht1"], PRIME)
                eng.wait_ge(s_edges, 48)
                if fast:
                    one_hot_out(0, 0)
                else:
                    for k in range(3):
                        index(0, k, k, 0, dst_i)

                def step0(s, k, i, more):
                    if not fast and more(3):
                        index(0, s + 3, k + 3, i, dst_i)
                    if fast and more(1):
                        one_hot_out(s + 1, k + 1)
                    comb_out(0, s, k)
                sweep(eng, step0)
                norm(0)
                for k in range(3):
                    index(1, k, k, 0, src_i)
                for k in range(2):
                    hidden(k, k)

                def step1(s, k, i, more):
                    if more(3):
                        index(1, s + 3, k + 3, i, src_i)
                    if more(2):
                        hidden(s + 2, k + 2)
                    if not fast:
                        comb_out(1, s, k)
                sweep(eng, step1)
                norm(1)
            both(eng, program)

        @block.tensor
        def _(eng):
            eng.wait_ge(s_const, 13)
            eng.wait_ge(s_step, 4)
            nc.tensor.matmul(ps_a[0:1, 0:1], ext[:, 4:5], onescol[:, :], start=True, stop=True).then_inc(s_flagps, 1)

            def one_hot_turn(s, k):
                eng.wait_ge(L[0]["oh"], after(s))
                eng.wait_ge(L[0]["oht"], after(s - 1))
                for t in range(T):
                    last = nc.tensor.transpose(oht_ps[:, t, :], oh_b[:, k % 2, t, :], identb[:, :])
                last.then_inc(L[0]["oht_ps"], 1)

            def keys(n, s, k):
                eng.wait_ge(L[n]["keyf"], after(s))
                eng.wait_ge(L[n]["key_free"], after(s - 1))
                if n == 1:
                    eng.wait_ge(L[1]["comb"], after(s - 1))
                for t in range(T):
                    last = nc.tensor.transpose((key_ps0 if n == 0 else key_ps1)[:, t, :],
                                               keyf[:, k % 2, t:t + 1].to_broadcast([P, P]), ident[:, :])
                last.then_inc(L[n]["key_ps"], 1)

            def pick(s, k, i):
                eng.wait_ge(L[0]["oht"], after(s))
                eng.wait_ge(s_xwin[k % SLOTS], uses(i, k) * 16 + 16)
                eng.wait_ge(L[0]["msg"], after(s - 1))
                for t in range(T):
                    last = nc.tensor.matmul(x_ps[:, t, :], oht[:, k % 2, t, :], xwin[:, k % SLOTS, :],
                                            start=True, stop=True)
                last.then_inc(L[0]["x_ps"], 1)

            def combine(n, s, k):
                eng.wait_ge(L[n]["msg"], after(s))
                eng.wait_ge(L[n]["same"], after(s))
                eng.wait_ge(L[n]["comb"], after(s - 1))
                if n == 1:
                    eng.wait_ge(L[1]["key_free"], after(s))
                for t in range(T):
                    last = nc.tensor.matmul((comb_ps0 if n == 0 else comb_ps1)[:, t, :],
                                            same[:, k % 2, t, :], msg[:, k % 2, t, :], start=True, stop=True)
                last.then_inc(L[n]["comb_ps"], 1)

            def hidden(s, k, i):
                b = k // CHUNK % 2
                if k % CHUNK == 0:
                    eng.wait_ge(s_hs[b], (i + k // U) * (16 * NSPLIT) + 16 * NSPLIT)
                for c in range(2):
                    eng.wait_ge(L[1][f"ht{c}"], after(s - 1))
                    nc.tensor.matmul(ps_h[:, c, :], w1k[:, c * P:(c + 1) * P],
                                     hs[:, b, k % CHUNK * SB:(k % CHUNK + 1) * SB], start=True, stop=True)\
                        .then_inc(L[1][f"hps{c}"], 1)

            def weights(s, k):
                for c in range(2):
                    eng.wait_ge(L[1][f"ht{c}"], after(s))
                eng.wait_ge(L[1]["pb"], after(s - 2))
                for t in range(T):
                    at = 2 * (k % 2) + t // 2
                    for c in range(2):
                        last = nc.tensor.matmul(ps_w[:, at, t % 2 * HID:(t % 2 + 1) * HID],
                                                hT[:, k % 2, c, t * P:(t + 1) * P], w2s[:, c, :],
                                                start=(c == 0), stop=(c == 1))
                last.then_inc(L[1]["w_ps"], 1)

            def window_sum(s, k):
                eng.wait_ge(L[1]["msg"], after(s))
                eng.wait_ge(L[1]["added"], after(s - 1))
                for t in range(T):
                    last = nc.tensor.matmul(ps_a[0:D, 0:WIN], msg[:, k % 2, t, :], oh[:, k % 2, t, :],
                                            start=(t == 0), stop=(t == T - 1))
                last.then_inc(L[1]["acc"], 1)

            def program(fast):
                for name in ("oht_ps", "key_ps", "x_ps", "comb_ps"):
                    eng.sem_inc(L[0][name], PRIME)
                for name in ("hps0", "hps1", "w_ps", "acc", "key_ps", "comb_ps"):
                    eng.sem_inc(L[1][name], PRIME)
                if fast:
                    one_hot_turn(0, 0)
                keys(0, 0, 0)

                def step0(s, k, i, more):
                    if more(1):
                        if fast:
                            one_hot_turn(s + 1, k + 1)
                        keys(0, s + 1, k + 1)
                    if fast:
                        pick(s, k, i)
                    combine(0, s, k)
                sweep(eng, step0)
                eng.wait_ge(s_w1k, 1)
                eng.wait_ge(s_w2, 1)
                eng.wait_ge(s_normed[0], 1)
                hidden(0, 0, 0)
                hidden(1, 1, 0)
                weights(0, 0)

                def step1(s, k, i, more):
                    if more(2):
                        hidden(s + 2, k + 2, i)
                    if more(1):
                        weights(s + 1, k + 1)
                    if fast:
                        window_sum(s, k)
                    else:
                        keys(1, s, k)
                        combine(1, s, k)
                sweep(eng, step1)
                if fast:
                    eng.wait_ge(L[1]["added"], after(NSB - 1))
                    eng.wait_ge(L[1]["pb"], after(NSB - 1))
                    acc_v = big[0:D, 0:NP].rearrange("f (p j) -> f j p", j=NJ)
                    for j in range(NJ):
                        if j % 16 == 0 and j >= 64:
                            eng.wait_ge(s_turned_read, j // 16 - 3)
                        last = nc.tensor.transpose(ps_w[:, j // 16 % 4, j % 16 * D:(j % 16 + 1) * D],
                                                   acc_v[:, j, :], ident[0:D, 0:D])
                        if j % 16 == 15 or j == NJ - 1:
                            last.then_inc(s_turned, 1)
            both(eng, program)

        @block.vector
        def _(eng):
            V = nc.vector
            eng.wait_ge(s_edges, 48)
            rel_v = rel[:, :].rearrange("p (s t) -> p s t", t=T)
            V.tensor_tensor(rel_v, dst_i[:, :].rearrange("p (s t) -> p s t", t=T),
                            spread(first_i[:, :], 2, T), ALU.subtract).then_inc(s_step, 1)
            eng.wait_ge(s_step, 1)
            V.tensor_reduce(ext[:, 0:1], rel[:, :], AX_X, ALU.max).then_inc(s_step, 1)
            V.tensor_reduce(ext[:, 1:2], rel[:, :], AX_X, ALU.min).then_inc(s_step, 1)
            eng.wait_ge(s_step, 3)
            V.tensor_scalar(ext[:, 2:3], ext[:, 0:1], WIN - 0.5, None, ALU.is_gt).then_inc(s_ext, 1)
            V.tensor_scalar(ext[:, 3:4], ext[:, 1:2], -0.5, None, ALU.is_lt).then_inc(s_ext, 1)
            eng.wait_ge(s_ext, 2)
            V.tensor_tensor(ext[:, 4:5], ext[:, 2:3], ext[:, 3:4], ALU.add).then_inc(s_step, 1)
            eng.wait_ge(s_flagps, 1)
            V.tensor_scalar(flag_i[:, :], ps_a[0:1, 0:1], 0.5, None, ALU.is_gt).then_inc(s_flag, 1)

            eng.wait_ge(s_wload, 16 * 10)
            eng.wait_ge(s_const, 13)
            w = lambda j: w1s[:, j, :]
            chain = [0]

            def link(ins):
                chain[0] += 1
                ins.then_inc(s_link, 1)
                eng.wait_ge(s_link, chain[0])
            link(V.tensor_copy(w1p[:, 0, :], w(0)))
            link(V.tensor_tensor(w(1), w(0), w1p[:, 0, :], ALU.subtract))
            link(V.tensor_copy(w1p[:, 1, :], w(1)))
            link(V.tensor_tensor(w(2), w(1), w1p[:, 1, :], ALU.subtract))
            link(V.tensor_copy(w1p[:, 2, :], w(2)))
            link(V.tensor_scalar(w(3), w1p[:, 0, :], w1m[:, 0:1], None, ALU.mult))
            link(V.scalar_tensor_tensor(w(4), w1p[:, 1, :], w1m[:, 1:2], w(3), ALU.mult, ALU.add))
            V.scalar_tensor_tensor(w1k[:, :], w1p[:, 2, :], w1m[:, 2:3], w(4), ALU.mult, ALU.add)\
                .then_inc(s_w1k, 1)
            scale = (1.0 / HID ** 0.5) * (1.0 / 128.0) ** 0.5 / (E / N) ** 0.5
            link(V.tensor_scalar(w2s[:, :, :], w2s[:, :, :], scale, None, ALU.mult))
            V.tensor_scalar(w2s[:, :, 2 * MUL * MUL:3 * MUL * MUL], w2s[:, :, 2 * MUL * MUL:3 * MUL * MUL],
                            1.0 / 3.0 ** 0.5, None, ALU.mult).then_inc(s_w2, 1)

            for q in range(8):
                eng.wait_ge(s_esa, q + 1)
                V.tensor_tensor(es_r, es_f, es_b[0], ALU.subtract).then_inc(s_esr, 1)
                eng.wait_ge(s_esb, q + 1)
                V.tensor_tensor(es_b[2], es_r, es_b[1], ALU.subtract).then_inc(s_esc, 1)

            def key_cast(n, s, k, ids):
                V.tensor_copy(keyf[:, k % 2, :], ids[:, bass.ds(s * T, T)]).then_inc(L[n]["keyf"], 1)

            def one_hot(n, s, k):
                V.tensor_tensor((oh_b if n == 0 else oh)[:, k % 2, :, :], spread(iota_ps, 1, T),
                                spread(rel[:, bass.ds(s * T, T)], 2, WIN), ALU.is_equal)\
                    .then_inc(L[n]["oh"], 1)

            def dedupe(n, s, k):
                b = k % 2
                key_ps = key_ps0 if n == 0 else key_ps1
                eng.wait_ge(L[n]["keyf"], after(s))
                eng.wait_ge(L[n]["key_ps"], after(s))
                eng.wait_ge(L[n]["comb"], after(s - 2))
                V.tensor_tensor(same[:, b, :, :], key_ps, spread(keyf[:, b, :], 2, P), ALU.is_equal)\
                    .then_inc(L[n]["same"], 1)
                for t in range(T):
                    last = V.scalar_tensor_tensor(junk[:, t, :], key_ps[:, t, :], keyf[:, b, t:t + 1], tri[:, :],
                                                  ALU.is_equal, ALU.mult, accum_out=dup[:, b, 0, t:t + 1])
                last.then_inc(L[n]["key_free"], 1)
                V.tensor_scalar(dup[:, b, 1, :], keyf[:, b, :], -1.0, trash[:, :], ALU.mult, ALU.add)\
                    .then_inc(L[n]["scaled"], 1)
                eng.wait_ge(L[n]["key_free"], after(s))
                eng.wait_ge(L[n]["scaled"], after(s * 2))
                V.scalar_tensor_tensor(dup[:, b, 2, :], dup[:, b, 0, :], 0.5, dup[:, b, 1, :],
                                       ALU.is_gt, ALU.mult).then_inc(L[n]["scaled"], 1)
                eng.wait_ge(L[n]["scaled"], after(s * 2 + 1))
                eng.wait_ge(L[n]["retired"], s * T + T)
                V.tensor_tensor(sidx[:, k % SLOTS, :], dup[:, b, 2, :], keyf[:, b, :], ALU.add)\
                    .then_inc(L[n]["sidx"], 1)

            def message(s, k, i, fast):
                if fast:
                    eng.wait_ge(L[0]["x_ps"], after(s))
                    rows = x_ps
                else:
                    eng.wait_ge(s_gat[0][k % SLOTS], uses(i, k) * 16 * T + 16 * T)
                    rows = gat[:, k % SLOTS, :, :]
                V.tensor_tensor(msg[:, k % 2, :, :], rows, spread(wgt[:, bass.ds(s * T, T)], 2, D), ALU.mult)\
                    .then_inc(L[0]["msg"], 1)

            def turned(n, s, k):
                key_cast(n, s, k, src_i)

            def sh_at(s):
                return sh_sb[:, bass.ds(s * (4 * T), 4 * T)].rearrange("p (t c) -> p t c", t=T)

            def pre(s, k, i):
                q = k % SLOTS
                eng.wait_ge(s_gat[1][q], uses(i, k) * 16 * T + 16 * T)
                V.tensor_tensor(vv[:, :, :, :], gat[:, q, :, MUL:D].rearrange("p t (u i) -> p t u i", i=3),
                                spread(sh_at(s)[:, :, 1:4], 2, MUL), ALU.mult).then_inc(L[1]["pre"], 1)

            def tensor_product(s, k):
                q = k % SLOTS
                wv = ps_w[:, 2 * (k % 2):2 * (k % 2) + 2, :].rearrange("p b (t n) -> p (b t) n", t=2)
                m2 = MUL * MUL
                eng.wait_ge(L[1]["w_ps"], after(s))
                V.tensor_tensor(prod_s[:, :, :, :], wv[:, :, 0:2 * m2].rearrange("p t (u w) -> p t u w", u=MUL),
                                spread(gat[:, q, :, 0:MUL], 3, 2 * MUL), ALU.mult).then_inc(L[1]["ps"], 1)
                eng.wait_ge(L[1]["pre"], after(s))
                V.tensor_reduce(vdot[:, :, :], vv[:, :, :, :], AX_X, ALU.add).then_inc(L[1]["dot"], 1)
                vec = gat[:, q, :, MUL:D].rearrange("p t (u i) -> p t u i", i=3)
                for c in range(3):
                    last = V.tensor_tensor(prod_v[:, c, :, :, :],
                                           wv[:, :, 3 * m2:4 * m2].rearrange("p t (u w) -> p t u w", u=MUL),
                                           spread(vec[:, :, :, c], 3, MUL), ALU.mult)
                last.then_inc(L[1]["pv"], 1)
                eng.wait_ge(L[1]["dot"], after(s))
                V.tensor_tensor(prod_b[:, :, :, :], wv[:, :, 2 * m2:3 * m2].rearrange("p t (u w) -> p t u w", u=MUL),
                                spread(vdot[:, :, :], 3, MUL), ALU.mult).then_inc(L[1]["pb"], 1)
                eng.wait_ge(L[1]["ps"], after(s))
                for c, at in ((0, 0), (1, 4)):
                    last = V.tensor_reduce(red[:, :, at, :],
                                           prod_s[:, :, :, c * MUL:(c + 1) * MUL].rearrange("p t u w -> p t w u"),
                                           AX_X, ALU.add)
                last.then_inc(L[1]["rs"], 1)
                eng.wait_ge(L[1]["pv"], after(s))
                for c in range(3):
                    last = V.tensor_reduce(red[:, :, 1 + c, :],
                                           prod_v[:, c, :, :, :].rearrange("p t u w -> p t w u"), AX_X, ALU.add)
                last.then_inc(L[1]["rv"], 1)
                eng.wait_ge(L[1]["pb"], after(s))
                V.tensor_reduce(side[:, :, 0, :], prod_b[:, :, :, :].rearrange("p t u w -> p t w u"),
                                AX_X, ALU.add).then_inc(L[1]["rb"], 1)
                eng.wait_ge(L[1]["rs"], after(s))
                V.tensor_tensor(side[:, :, 1:4, :], spread(red[:, :, 4, :], 2, 3),
                                spread(sh_at(s)[:, :, 1:4], 3, MUL), ALU.mult).then_inc(L[1]["cross"], 1)
                eng.wait_ge(L[1]["rv"], after(s))
                V.tensor_tensor(red[:, :, 0:4, :], red[:, :, 0:4, :], spread(spread(sh_at(s)[:, :, 0], 2, 4), 3, MUL),
                                ALU.mult).then_inc(L[1]["outer"], 1)
                eng.wait_ge(L[1]["cross"], after(s))
                eng.wait_ge(L[1]["outer"], after(s))
                eng.wait_ge(L[1]["rb"], after(s))
                V.tensor_tensor(msg[:, k % 2, :, :].rearrange("p t (c w) -> p t c w", c=4),
                                red[:, :, 0:4, :], side[:, :, :, :], ALU.add).then_inc(L[1]["msg"], 1)

            def add_window(s, k):
                base = eng.value_load(first_i[0:1, bass.ds(s, 1)], min_val=0, max_val=N - 1)
                eng.wait_ge(L[1]["acc"], after(s))
                eng.wait_ge(L[1]["added"], after(s - 1))
                V.tensor_tensor(big[0:D, bass.ds(base, WIN)], ps_a[0:D, 0:WIN], big[0:D, bass.ds(base, WIN)],
                                ALU.add).then_inc(L[1]["added"], 1)

            def table_sum():
                for t in range(1, T):
                    V.tensor_tensor(work[:, :], big[:, 0:NJ * D] if t == 1 else work[:, :],
                                    big[:, t * NJ * D:(t + 1) * NJ * D], ALU.add).then_inc(s_link, 1)
                    chain[0] += 1
                    eng.wait_ge(s_link, chain[0])

            def norm(n, dest):
                zv = work[:, :].rearrange("p (j f) -> p j f", f=D)
                link(V.tensor_reduce(stat[:, 0, :], zv, AX_X, ALU.add))
                link(V.tensor_scalar(stat[:, 3, :], stat[:, 0, :], -1.0 / D, None, ALU.mult))
                V.tensor_tensor(zv, zv, spread(stat[:, 3, :], 2, D), ALU.add).then_inc(s_centred[n], 1)
                eng.wait_ge(s_squared[n], 1)
                V.tensor_reduce(stat[:, 1, :], big[:, 0:NJ * D].rearrange("p (j f) -> p j f", f=D),
                                AX_X, ALU.add).then_inc(s_summed[n], 1)
                eng.wait_ge(s_std[n], 1)
                link(V.reciprocal(stat[:, 3, :], stat[:, 2, :]))
                V.tensor_tensor(dest[:, :].rearrange("p (j f) -> p j f", f=D), zv,
                                spread(stat[:, 3, :], 2, D), ALU.mult).then_inc(s_normed[n], 1)

            def program(fast):
                saved = chain[0]
                for name in ("keyf", "oh", "same", "key_free", "scaled", "sidx", "msg"):
                    eng.sem_inc(L[0][name], PRIME)
                for name in ("keyf", "oh", "same", "key_free", "scaled", "sidx", "msg", "pre", "dot", "ps",
                             "pv", "pb", "rs", "rv", "rb", "cross", "outer", "added"):
                    eng.sem_inc(L[1][name], PRIME)
                eng.wait_ge(s_iotab, 1)
                eng.wait_ge(s_w, 16)
                key_cast(0, 0, 0, src_i)
                if fast:
                    one_hot(0, 0, 0)
                dedupe(0, 0, 0)

                def step0(s, k, i, more):
                    if more(1):
                        key_cast(0, s + 1, k + 1, src_i)
                        if fast:
                            one_hot(0, s + 1, k + 1)
                        dedupe(0, s + 1, k + 1)
                    message(s, k, i, fast)
                sweep(eng, step0)
                eng.wait_ge(s_tab, 16 * T)
                table_sum()
                norm(0, x1)
                if fast:
                    link(V.memset(big[0:D, :], 0.0))
                eng.wait_ge(s_sh, 16)

                def step1(s, k, i, more, head=False):
                    if fast:
                        one_hot(1, s, k)
                    else:
                        key_cast(1, s, k, dst_i)
                        dedupe(1, s, k)
                    pre(s, k, i)
                    tensor_product(s, k)
                    if fast:
                        add_window(s, k)
                sweep(eng, step1)
                if fast:
                    for g in range(-(-NJ // 16)):
                        eng.wait_ge(s_turned, g + 1)
                        j0, j1 = 16 * g, min(NJ, 16 * g + 16)
                        part = ps_w[:, g % 4, 0:(j1 - j0) * D].rearrange("p (j f) -> p j f", f=D)
                        last = add_nodes(j0, j1, part)
                        last.then_inc(s_turned_read, 1)
                    eng.wait_ge(s_turned_read, -(-NJ // 16))
                else:
                    eng.wait_ge(s_tab, 32 * T)
                    table_sum()
                    link(V.tensor_copy(big[:, 0:NJ * D], work[:, :]))
                    link(add_nodes(0, NJ, big[:, 0:NJ * D].rearrange("p (j f) -> p j f", f=D)))
                norm(1, work)
                chain[0] = saved

            def add_nodes(j0, j1, part):
                xv = x1[:, j0 * D:j1 * D].rearrange("p (j f) -> p j f", f=D)
                wv = work[:, j0 * D:j1 * D].rearrange("p (j f) -> p j f", f=D)
                V.tensor_tensor(wv[:, :, 0:MUL], xv[:, :, 0:MUL], part[:, :, 0:MUL], ALU.add)
                return V.tensor_tensor(wv[:, :, MUL:D].rearrange("p j (w i) -> p j w i", i=3),
                                       xv[:, :, MUL:D].rearrange("p j (w i) -> p j w i", i=3),
                                       part[:, :, MUL:D].rearrange("p j (i w) -> p j w i", i=3), ALU.add)
            both(eng, program)




def kernel(x, src, dst, edge_attr_4, edge_attr_8, edge_weight, L1_gnn_fc_w1, L1_gnn_fc_w2):
    import numpy as np
    import concourse.bacc as bacc
    from concourse.bass_utils import run_bass_kernel_spmd

    def edges(a, how="constant"):
        a = np.pad(np.asarray(a), [(0, EP - E)] + [(0, 0)] * (a.ndim - 1), mode=how)
        return a.reshape(NSB, P, T, -1)

    def on_partitions(a):
        return np.ascontiguousarray(a.transpose(1, 0, 2, 3).reshape(P, -1))

    targets = edges(dst, "edge")
    w2 = np.asarray(L1_gnn_fc_w2).reshape(HID, 4, MUL, MUL)
    w2 = np.concatenate([w2[:, 0:3:2].transpose(0, 2, 1, 3).reshape(HID, -1),
                         w2[:, 1].reshape(HID, -1), w2[:, 3].reshape(HID, -1)], axis=1)
    arrays = {
        "x": np.pad(np.asarray(x), [(0, ROWS - N), (0, 0)]),
        "src": on_partitions(edges(src)),
        "dst": on_partitions(targets),
        "first": np.ascontiguousarray(np.broadcast_to(targets[:, 0, 0, 0], (P, NSB))),
        "weight": on_partitions(edges(edge_weight)),
        "sh": on_partitions(edges(edge_attr_4)),
        "es": np.ascontiguousarray(edges(edge_attr_8).transpose(3, 0, 2, 1).reshape(BASIS, EP)),
        "w1": np.ascontiguousarray(L1_gnn_fc_w1),
        "w2": np.ascontiguousarray(w2),
    }
    nc = bacc.Bacc("TRN2", target_bir_lowering=False, num_devices=1)
    args = [nc.dram_tensor(name, a.shape, mybir.dt.from_np(a.dtype), kind="ExternalInput").ap()
            for name, a in arrays.items()]
    out = nc.dram_tensor("out", (NP, D), F32, kind="ExternalOutput").ap()
    gnn_kernel(nc, *args, out)
    r = run_bass_kernel_spmd(nc, [arrays], core_ids=[0])
    return r.results[0]["out"][0:N]
```

```python
from contextlib import ExitStack

import concourse.bass as bass
from concourse import mybir

F32 = mybir.dt.float32
BF16 = mybir.dt.bfloat16
I32 = mybir.dt.int32
ALU = mybir.AluOpType
ACT = mybir.ActivationFunctionType
AX_X = mybir.AxisListType.X

P = 128
N, E, D = 12500, 200000, 32
MUL, BASIS, HID = 8, 8, 256
T = 4
SB = P * T
U = 8
TURNS = -(-E // (SB * U))
NSB = TURNS * U
EP = NSB * SB
NJ = -(-N // P)
NP = P * NJ
ROWS = NP + P
WIN = P
SLOTS = 4
RING = 8
PRIME = 6
EPS = 1e-5
ESCOLS = 8 * EP // P
ESPART = ESCOLS // TURNS
NSPLIT = 3
KROWS = NSPLIT * NSPLIT * BASIS
CHUNK = 4


def after(s):
    return s + (1 + PRIME)


def spread(ap, axis, count):
    ap = ap.unsqueeze(axis)
    shape = list(ap.shape)
    shape[axis] = count
    return ap.to_broadcast(shape)


def gnn_kernel(nc, x, src, dst, first, weight, sh, es, w1, w2, out):
    tables = [nc.dram_tensor(f"table{t}", [ROWS, D], F32, kind="Internal").ap() for t in range(T)]
    nodes1 = nc.dram_tensor("nodes1", [NP, D], F32, kind="Internal").ap()
    x_split = nc.dram_tensor("x_split", [ROWS, NSPLIT * D], BF16, kind="Internal").ap()
    es_split = nc.dram_tensor("es_split", [NSPLIT * BASIS, EP], BF16, kind="Internal").ap()

    ctx = ExitStack()
    with ctx:
        def sb(name, shape, dt=F32):
            return ctx.enter_context(nc.sbuf_tensor(name, shape, dt))

        def sem(name):
            return ctx.enter_context(nc.semaphore(name))

        src_i = sb("src_i", [P, NSB * T], I32)
        dst_i = sb("dst_i", [P, NSB * T], I32)
        first_i = sb("first_i", [P, NSB], I32)
        rel = sb("rel", [P, NSB * T])
        nrel = sb("nrel", [P, NSB * T])
        wgt = sb("wgt", [P, NSB * T])
        sh_sb = sb("sh_sb", [P, NSB * T * 4])
        big = sb("big", [P, ROWS])
        x1 = sb("x1", [P, NJ * D])
        work = sb("work", [P, NJ * D])
        stat = sb("stat", [P, 4, NJ])
        iota_sb = sb("iota_sb", [P, P])
        tri = sb("tri", [P, P])
        ident = sb("ident", [P, P])
        identb = sb("identb", [P, P], BF16)
        onescol = sb("onescol", [P, 1])
        zeros = sb("zeros", [P, ROWS // P * D // 3])
        trash = sb("trash", [P, 1])
        eps = sb("eps", [P, 1])
        ext = sb("ext", [P, 8])
        flag_i = sb("flag_i", [1, 1], I32)
        w1s = sb("w1s", [KROWS, 6, HID])
        w1p = sb("w1p", [KROWS, NSPLIT, HID], BF16)
        w1m = sb("w1m", [KROWS, NSPLIT])
        w1k = sb("w1k", [KROWS, HID], BF16)
        w2s = sb("w2s", [P, 2, HID])
        keyf = sb("keyf", [P, 2, T])
        oh_b = sb("oh_b", [P, 2, T, WIN], BF16)
        oht = sb("oht", [P, 2, T, P], BF16)
        oh = sb("oh", [P, 2, T, WIN])
        same = sb("same", [P, SLOTS, T, P])
        sq = sb("sq", [P, T, WIN])
        junk = sb("junk", [P, T, P])
        dup = sb("dup", [P, 2, 3, T])
        xwin = sb("xwin", [P, SLOTS, NSPLIT * D], BF16)
        msg = sb("msg", [P, 2, T, D])
        comb = sb("comb", [P, RING, T, D])
        sidx = sb("sidx", [P, RING, T], I32)
        gidx = sb("gidx", [P, SLOTS, T], I32)
        gat = sb("gat", [P, SLOTS, T, D])
        hs = sb("hs", [KROWS, 2, CHUNK * SB], BF16)
        hT = sb("hT", [P, 2, 2, SB])
        vv = sb("vv", [P, T, MUL, 3])
        vdot = sb("vdot", [P, T, MUL])
        prod_s = sb("prod_s", [P, T, MUL, 2 * MUL])
        prod_v = sb("prod_v", [P, T, 4, MUL, MUL])
        red = sb("red", [P, T, 9, MUL])

        es_sb = sb("es_sb", [P, 2 * ESPART])
        es_b = [sb(f"es_b{m}", [P, ESPART], BF16) for m in range(NSPLIT)]

        ps_w = ctx.enter_context(nc.psum_tensor("ps_w", [P, 4, 512], F32))
        ps_h = ctx.enter_context(nc.psum_tensor("ps_h", [P, 2, 512], F32))
        ps_d = ctx.enter_context(nc.psum_tensor("ps_d", [P, 512], F32))
        ps_a = ctx.enter_context(nc.psum_tensor("ps_a", [P, 512], F32))
        XC = ROWS // P * D
        x_f, x_r = big[:, 0:XC], big[:, XC:2 * XC]
        x_parts = big[:, 2 * XC:2 * XC + NSPLIT * XC // 2].bitcast(BF16)
        x_b = x_parts.rearrange("p (r m f) -> p m r f", m=NSPLIT, f=D)
        es_f = es_sb[:, 0:ESPART]
        es_r = es_sb[:, ESPART:2 * ESPART]
        iota_ps = ps_d[:, 0:P]
        oht_ps = ps_w[:, 0, 0:SB // 2].bitcast(BF16).rearrange("p (t e) -> p t e", t=T)
        x_ps = ps_w[:, 1, 0:T * D].rearrange("p (t f) -> p t f", t=T)
        key_ps0 = ps_w[:, 2, :].rearrange("p (t e) -> p t e", t=T)
        comb_ps0 = ps_w[:, 3, 0:T * D].rearrange("p (t f) -> p t f", t=T)
        key_ps1 = ps_a[:, :].rearrange("p (t e) -> p t e", t=T)
        comb_ps1 = ps_a[:, 0:T * D].rearrange("p (t f) -> p t f", t=T)

        s_edges, s_w, s_sh, s_wload, s_init = map(sem, ("s_edges", "s_w", "s_sh", "s_wload", "s_init"))
        s_const, s_iotab, s_zero, s_step, s_flag, s_flagps = map(
            sem, ("s_const", "s_iotab", "s_zero", "s_step", "s_flag", "s_flagps"))
        s_xin, s_xa, s_xr, s_xb, s_xc, s_xsplit = map(
            sem, ("s_xin", "s_xa", "s_xr", "s_xb", "s_xc", "s_xsplit"))
        s_nrel, s_esdone = sem("s_nrel"), sem("s_esdone")
        s_w1k, s_w2, s_link, s_ext = sem("s_w1k"), sem("s_w2"), sem("s_link"), sem("s_ext")
        s_es, s_esa, s_esb, s_esr, s_esc, s_esout = map(
            sem, ("s_es", "s_esa", "s_esb", "s_esr", "s_esc", "s_esout"))
        s_tab = sem("s_tab")
        s_x1out, s_out = sem("s_x1out"), sem("s_out")
        s_turned, s_turned_read = sem("s_turned"), sem("s_turned_read")
        s_landed = [sem(f"s_landed{n}") for n in range(2)]
        s_centred = [sem(f"s_centred{n}") for n in range(2)]
        s_squared = [sem(f"s_squared{n}") for n in range(2)]
        s_summed = [sem(f"s_summed{n}") for n in range(2)]
        s_std = [sem(f"s_std{n}") for n in range(2)]
        s_normed = [sem(f"s_normed{n}") for n in range(2)]

        def layer_sems(n):
            return {name: sem(f"{name}{n}") for name in (
                "keyf", "oh", "oht_ps", "oht", "key_ps", "same", "key_free", "sidx", "x_ps",
                "msg", "comb_ps", "comb", "retired", "gidx", "hps0", "hps1", "ht0", "ht1",
                "w_ps", "w_free", "pre", "dot", "ps", "pv", "rs", "rv", "scaled",
                "cross", "outer", "sq", "asked", "acc", "added")}
        L = [layer_sems(0), layer_sems(1)]
        s_xwin = [sem(f"s_xwin{q}") for q in range(SLOTS)]
        s_gat = [[sem(f"s_gat{n}_{q}") for q in range(SLOTS)] for n in range(2)]
        s_scat = [[sem(f"s_scat{n}_{t}") for t in range(T)] for n in range(2)]
        s_hs = [sem(f"s_hs{b}") for b in range(2)]

        block = ctx.enter_context(nc.Block())

        def sweep(eng, step, head=0):
            for i in range(head):
                for k in range(U):
                    step(i * U + k, k, i, lambda d: True)
            with eng.Fori(head, TURNS - 1) as i:
                for k in range(U):
                    step(i * U + k, k, i, lambda d: True)
            for k in range(U):
                step((TURNS - 1) * U + k, k, TURNS - 1, lambda d: k + d < U)

        def uses(i, k):
            return i * (U // SLOTS) + k // SLOTS

        def both(eng, program):
            eng.wait_ge(s_flag, 1)
            flag = eng.value_load(flag_i[0:1, 0:1], min_val=0, max_val=1)
            with eng.If(flag == 0):
                program(True)
            with eng.Else():
                program(False)

        @block.sync
        def _(eng):
            eng.dma_start(x_f, x.rearrange("(p r) f -> p (r f)", p=P)).then_inc(s_xin, 16)
            eng.dma_start(dst_i[:, :], dst).then_inc(s_edges, 16)
            eng.dma_start(first_i[:, :], first).then_inc(s_edges, 16)
            eng.dma_start(src_i[:, :], src).then_inc(s_edges, 16)
            eng.dma_start(wgt[:, :], weight).then_inc(s_w, 16)
            for q in range(NSPLIT * NSPLIT):
                eng.dma_start(w1s[q * BASIS:(q + 1) * BASIS, 0, :], w1).then_inc(s_wload, 16)
            eng.dma_start(w2s[:, :, :], w2.rearrange("(c p) n -> p c n", c=2)).then_inc(s_wload, 16)
            eng.dma_start(sh_sb[:, :], sh).then_inc(s_sh, 16)
            eng.dma_start(tables[0].rearrange("(p r) f -> p (r f)", p=P),
                          x.rearrange("(p r) f -> p (r f)", p=P)).then_inc(s_init, 16)
            eng.wait_ge(s_zero, 1)
            for t in range(1, T):
                eng.dma_start(tables[t].rearrange("(p a r) f -> p a (r f)", p=P, a=3),
                                      spread(zeros[:, :], 1, 3)).then_inc(s_init, 16)
            es_out = es_split.rearrange("(m r) (c n) -> m (r c) n", m=NSPLIT, c=P // BASIS)
            es_in = es.rearrange("r (c n) -> (r c) n", c=P // BASIS)

            def split_io(k, i):
                if k == 0:
                    eng.wait_ge(s_esdone, i * 2 + 1)
                    eng.dma_start(es_f, es_in[:, bass.ds(i * ESPART, ESPART)]).then_inc(s_es, 16)
                if k == U - 1:
                    eng.wait_ge(s_esc, i + 1)
                    eng.sem_inc(s_esdone, 1)
                    for m in range(NSPLIT):
                        eng.dma_start(es_out[m, :, bass.ds(i * ESPART, ESPART)], es_b[m][:, :]).then_inc(s_esout, 16)
                    eng.wait_ge(s_esout, i * (16 * NSPLIT) + 16 * NSPLIT)
                    eng.sem_inc(s_esdone, 1)

            def load_tables():
                for t in range(T):
                    eng.dma_start(big[:, t * NJ * D:(t + 1) * NJ * D],
                                  tables[t][0:NP, :].rearrange("(p r) f -> p (r f)", p=P)).then_inc(s_tab, 16)

            def program(fast):
                def window(s, k, i, more):
                    if fast:
                        base = eng.value_load(first_i[0:1, bass.ds(s, 1)], min_val=0, max_val=N - 1)
                        eng.wait_ge(L[0]["x_ps"], after(s - SLOTS))
                        eng.dma_start(xwin[:, k % SLOTS, :], x_split[bass.ds(base, WIN), :]).then_inc(s_xwin[k % SLOTS], 16)
                    split_io(k, i)
                eng.wait_ge(s_xc, 1)
                eng.dma_start(x_split.rearrange("(p r) f -> p (r f)", p=P), x_parts).then_inc(s_xsplit, 16)
                eng.wait_ge(s_edges, 48)
                eng.wait_ge(s_xsplit, 16)
                eng.sem_inc(s_esdone, 1)
                sweep(eng, window)
                eng.wait_ge(s_landed[0], 1)
                load_tables()
                eng.wait_ge(s_normed[0], 1)
                eng.dma_start(nodes1.rearrange("(p r) f -> p (r f)", p=P), x1[:, :]).then_inc(s_x1out, 16)
                if not fast:
                    eng.wait_ge(s_tab, 16 * T)
                    for t in range(T):
                        eng.dma_start(tables[t].rearrange("(p a r) f -> p a (r f)", p=P, a=3),
                                      spread(zeros[:, :], 1, 3)).then_inc(s_init, 16)

                def scalars(s, k, i, more):
                    if k % CHUNK:
                        return
                    eng.wait_ge(L[1]["hps1"], after(s - CHUNK - 1))
                    b = k // CHUNK
                    for m in range(NSPLIT):
                        eng.dma_start(hs[m * NSPLIT * BASIS:(m + 1) * NSPLIT * BASIS, b, :],
                                      es_split[:, bass.ds(s * SB, CHUNK * SB)]).then_inc(s_hs[b], 16)
                sweep(eng, scalars)
                if not fast:
                    eng.wait_ge(s_landed[1], 1)
                    load_tables()
                eng.wait_ge(s_normed[1], 1)
                eng.dma_start(out.rearrange("(p r) f -> p (r f)", p=P), work[:, :]).then_inc(s_out, 16)
                eng.wait_ge(s_x1out, 16)
                eng.wait_ge(s_out, 16)
            both(eng, program)

        @block.gpsimd
        def _(eng):
            nc.gpsimd.memset(zeros[:, :], 0.0).then_inc(s_zero, 1)
            nc.gpsimd.iota(iota_sb[:, :], pattern=[[1, P]], base=0, channel_multiplier=0,
                           allow_small_or_imprecise_dtypes=True).then_inc(s_const, 1)
            nc.gpsimd.iota(trash[:, :], pattern=[[0, 1]], base=NP, channel_multiplier=1,
                           allow_small_or_imprecise_dtypes=True).then_inc(s_const, 1)
            nc.gpsimd.memset(eps[:, :], EPS).then_inc(s_const, 1)
            nc.gpsimd.memset(onescol[:, :], 1.0).then_inc(s_const, 1)
            nc.gpsimd.memset(tri[:, :], 1.0).then_inc(s_const, 1)
            nc.gpsimd.memset(ident[:, :], 0.0).then_inc(s_const, 1)
            nc.gpsimd.memset(identb[:, :], 0.0).then_inc(s_const, 1)
            nc.gpsimd.memset(w1m[:, :], 1.0).then_inc(s_const, 1)
            eng.wait_ge(s_const, 8)
            nc.gpsimd.affine_select(out=tri[:, :], in_=tri[:, :], compare_op=ALU.is_gt, fill=0.0,
                                    base=0, pattern=[[-1, P]], channel_multiplier=1).then_inc(s_const, 1)
            for m in (ident, identb):
                nc.gpsimd.affine_select(out=m[:, :], in_=m[:, :], compare_op=ALU.not_equal, fill=1.0,
                                        base=0, pattern=[[-1, P]], channel_multiplier=1).then_inc(s_const, 1)
            nc.gpsimd.affine_select(out=w1m[:, :], in_=w1m[:, :], compare_op=ALU.is_ge, fill=0.0,
                                    base=0, pattern=[[-NSPLIT * BASIS, NSPLIT]],
                                    channel_multiplier=1).then_inc(s_const, 1)
            eng.wait_ge(s_const, 12)
            nc.gpsimd.affine_select(out=w1m[:, :], in_=w1m[:, :], compare_op=ALU.is_ge, fill=0.0,
                                    base=NSPLIT * BASIS - 1, pattern=[[NSPLIT * BASIS, NSPLIT]],
                                    channel_multiplier=-1).then_inc(s_const, 1)

            def gather(n, s, k, i, table):
                q = k % SLOTS
                eng.wait_ge(L[n]["gidx"], after(s))
                eng.wait_ge(L[n]["msg" if n == 0 else "pv"], after(s - SLOTS))
                eng.sem_inc(L[n]["asked"], 1)
                for t in range(T):
                    nc.gpsimd.indirect_dma_start(
                        out=gat[:, q, t, :], out_offset=None, in_=table,
                        in_offset=bass.IndirectOffsetOnAxis(ap=gidx[:, q, t:t + 1], axis=0),
                    ).then_inc(s_gat[n][q], 16)

            def first_one(s):
                return isinstance(s, int) and s == 0

            def scatter(n, s, k, head):
                q = k % RING
                eng.wait_ge(L[n]["comb"], after(s))
                eng.wait_ge(L[n]["sidx"], after(s))
                for t in range(T):
                    if head:
                        eng.wait_ge(s_init, 16 * T * (n + 1))
                    else:
                        eng.wait_ge(s_scat[n][t], s * 16)
                    eng.sem_inc(L[n]["retired"], 1)
                    nc.gpsimd.indirect_dma_start(
                        out=tables[t], out_offset=bass.IndirectOffsetOnAxis(ap=sidx[:, q, t:t + 1], axis=0),
                        in_=comb[:, q, t, :], in_offset=None, compute_op=ALU.add,
                    ).then_inc(s_scat[n][t], 16)

            def program(fast):
                eng.sem_inc(L[0]["retired"], (RING - 1) * T)
                if fast:
                    sweep(eng, lambda s, k, i, more: scatter(0, s, k, first_one(s)), head=1)
                else:
                    for k in range(2):
                        gather(0, k, k, 0, x)

                    def step(s, k, i, more):
                        if more(2):
                            gather(0, s + 2, k + 2, i, x)
                        scatter(0, s, k, first_one(s))
                    sweep(eng, step, head=1)
                for t in range(T):
                    eng.wait_ge(s_scat[0][t], NSB * 16)
                eng.sem_inc(s_landed[0], 1)
                eng.wait_ge(s_x1out, 16)
                if fast:
                    sweep(eng, lambda s, k, i, more: gather(1, s, k, i, nodes1))
                else:
                    eng.sem_inc(L[1]["retired"], (RING - 1) * T)
                    for k in range(2):
                        gather(1, k, k, 0, nodes1)

                    def step(s, k, i, more):
                        if more(2):
                            gather(1, s + 2, k + 2, i, nodes1)
                        scatter(1, s, k, first_one(s))
                    sweep(eng, step, head=1)
                    for t in range(T):
                        eng.wait_ge(s_scat[1][t], NSB * 16)
                    eng.sem_inc(s_landed[1], 1)
            both(eng, program)

        @block.scalar
        def _(eng):
            eng.wait_ge(s_const, 13)
            nc.scalar.activation(iota_ps, iota_sb[:, :], ACT.Copy).then_inc(s_iotab, 1)
            x_rows = [v.rearrange("p (r f) -> p r f", f=D) for v in (x_f, x_r)]
            eng.wait_ge(s_xin, 16)
            nc.scalar.activation(x_b[:, 0], x_rows[0], ACT.Copy).then_inc(s_xa, 1)
            eng.wait_ge(s_xr, 1)
            nc.scalar.activation(x_b[:, 1], x_rows[1], ACT.Copy).then_inc(s_xb, 1)

            def split(k, i):
                if k == 1:
                    eng.wait_ge(s_es, i * 16 + 16)
                    nc.scalar.activation(es_b[0][:, :], es_f, ACT.Copy).then_inc(s_esa, 1)
                if k == 3:
                    eng.wait_ge(s_esr, i + 1)
                    nc.scalar.activation(es_b[1][:, :], es_r, ACT.Copy).then_inc(s_esb, 1)

            def index(n, s, k, i, ids):
                eng.wait_ge(L[n]["msg" if n == 0 else "pv"], after(s - SLOTS))
                nc.scalar.activation(gidx[:, k % SLOTS, :], ids[:, bass.ds(s * T, T)], ACT.Copy)\
                    .then_inc(L[n]["gidx"], 1)

            def one_hot_out(s, k):
                eng.wait_ge(L[0]["oht_ps"], after(s))
                eng.wait_ge(L[0]["x_ps"], after(s - 2))
                nc.scalar.activation(oht[:, k % 2, :, :], oht_ps, ACT.Copy).then_inc(L[0]["oht"], 1)

            def comb_out(n, s, k):
                eng.wait_ge(L[n]["comb_ps"], after(s))
                eng.wait_ge(L[n]["retired"], s * T + T)
                nc.scalar.activation(comb[:, k % RING, :, :], comb_ps0 if n == 0 else comb_ps1, ACT.Copy)\
                    .then_inc(L[n]["comb"], 1)

            def hidden(s, k):
                for c in range(2):
                    eng.wait_ge(L[1][f"hps{c}"], after(s))
                    nc.scalar.activation(hT[:, k % 2, c, :], ps_h[:, c, :], ACT.Relu,
                                         scale=(2.0 / BASIS) ** 0.5).then_inc(L[1][f"ht{c}"], 1)

            def one_hot(s, k):
                eng.wait_ge(L[1]["oh"], after(s - 1))
                for t in range(T):
                    last = nc.scalar.activation(sq[:, t, :], iota_sb[:, :], ACT.Square,
                                                bias=nrel[:, bass.ds(s * T + t, 1)])
                last.then_inc(L[1]["sq"], 1)
                eng.wait_ge(L[1]["sq"], after(s))
                eng.wait_ge(L[1]["acc"], after(s - 2))
                nc.scalar.activation(oh[:, k % 2, :, :], sq[:, :, :], ACT.Relu, scale=-1.0, bias=onescol[:, :])\
                    .then_inc(L[1]["oh"], 1)

            def norm(n):
                eng.wait_ge(s_centred[n], 1)
                nc.scalar.activation(big[:, 0:NJ * D], work[:, :], ACT.Square).then_inc(s_squared[n], 1)
                eng.wait_ge(s_summed[n], 1)
                nc.scalar.activation(stat[:, 2, :], stat[:, 1, :], ACT.Sqrt, bias=eps[:, :],
                                     scale=1.0 / D).then_inc(s_std[n], 1)

            def program(fast):
                eng.sem_inc(L[0]["comb"], PRIME)
                eng.sem_inc(L[0]["oht"], PRIME)
                eng.sem_inc(L[0]["gidx"], PRIME)
                eng.sem_inc(L[1]["gidx"], PRIME)
                eng.wait_ge(s_nrel, 1)
                eng.sem_inc(L[1]["comb"], PRIME)
                eng.sem_inc(L[1]["ht0"], PRIME)
                eng.sem_inc(L[1]["ht1"], PRIME)
                eng.sem_inc(L[1]["sq"], PRIME)
                eng.sem_inc(L[1]["oh"], PRIME)
                eng.wait_ge(s_edges, 48)
                if fast:
                    one_hot_out(0, 0)
                    one_hot_out(1, 1)
                else:
                    for k in range(3):
                        index(0, k, k, 0, dst_i)

                def step0(s, k, i, more):
                    if not fast and more(3):
                        index(0, s + 3, k + 3, i, dst_i)
                    if fast and more(2):
                        one_hot_out(s + 2, k + 2)
                    comb_out(0, s, k)
                    split(k, i)
                sweep(eng, step0)
                norm(0)
                for k in range(3):
                    index(1, k, k, 0, src_i)
                for k in range(2):
                    hidden(k, k)

                def step1(s, k, i, more):
                    if more(3):
                        index(1, s + 3, k + 3, i, src_i)
                    if more(2):
                        hidden(s + 2, k + 2)
                    if fast:
                        one_hot(s, k)
                    if not fast:
                        comb_out(1, s, k)
                sweep(eng, step1)
                norm(1)
            both(eng, program)

        @block.tensor
        def _(eng):
            eng.wait_ge(s_const, 13)
            eng.wait_ge(s_step, 4)
            nc.tensor.matmul(ps_a[0:1, 0:1], ext[:, 4:5], onescol[:, :], start=True, stop=True).then_inc(s_flagps, 1)

            def one_hot_turn(s, k):
                eng.wait_ge(L[0]["oh"], after(s))
                eng.wait_ge(L[0]["oht"], after(s - 1))
                for t in range(T):
                    last = nc.tensor.transpose(oht_ps[:, t, :], oh_b[:, k % 2, t, :], identb[:, :])
                last.then_inc(L[0]["oht_ps"], 1)

            def keys(n, s, k):
                eng.wait_ge(L[n]["keyf"], after(s))
                eng.wait_ge(L[n]["key_free"], after(s - 1))
                if n == 1:
                    eng.wait_ge(L[1]["comb"], after(s - 1))
                for t in range(T):
                    last = nc.tensor.transpose((key_ps0 if n == 0 else key_ps1)[:, t, :],
                                               keyf[:, k % 2, t:t + 1].to_broadcast([P, P]), ident[:, :])
                last.then_inc(L[n]["key_ps"], 1)

            def pick(s, k, i):
                eng.wait_ge(L[0]["oht"], after(s))
                eng.wait_ge(s_xwin[k % SLOTS], uses(i, k) * 16 + 16)
                eng.wait_ge(L[0]["msg"], after(s - 1))
                for t in range(T):
                    for m in range(NSPLIT):
                        last = nc.tensor.matmul(x_ps[:, t, :], oht[:, k % 2, t, :],
                                                xwin[:, k % SLOTS, m * D:(m + 1) * D],
                                                start=(m == 0), stop=(m == NSPLIT - 1))
                last.then_inc(L[0]["x_ps"], 1)

            def combine(n, s, k):
                eng.wait_ge(L[n]["msg"], after(s))
                eng.wait_ge(L[n]["same"], after(s))
                eng.wait_ge(L[n]["comb"], after(s - 1))
                if n == 1:
                    eng.wait_ge(L[1]["key_free"], after(s))
                for t in range(T):
                    last = nc.tensor.matmul((comb_ps0 if n == 0 else comb_ps1)[:, t, :],
                                            same[:, k % SLOTS, t, :], msg[:, k % 2, t, :], start=True, stop=True)
                last.then_inc(L[n]["comb_ps"], 1)

            def hidden(s, k, i):
                b = k // CHUNK % 2
                if k % CHUNK == 0:
                    eng.wait_ge(s_hs[b], (i + k // U) * (16 * NSPLIT) + 16 * NSPLIT)
                for c in range(2):
                    eng.wait_ge(L[1][f"ht{c}"], after(s - 1))
                    nc.tensor.matmul(ps_h[:, c, :], w1k[:, c * P:(c + 1) * P],
                                     hs[:, b, k % CHUNK * SB:(k % CHUNK + 1) * SB], start=True, stop=True)\
                        .then_inc(L[1][f"hps{c}"], 1)

            def weights(s, k):
                for c in range(2):
                    eng.wait_ge(L[1][f"ht{c}"], after(s))
                eng.wait_ge(L[1]["pv"], after(s - 2))
                for t in range(T):
                    at = 2 * (k % 2) + t // 2
                    for c in range(2):
                        last = nc.tensor.matmul(ps_w[:, at, t % 2 * HID:(t % 2 + 1) * HID],
                                                hT[:, k % 2, c, t * P:(t + 1) * P], w2s[:, c, :],
                                                start=(c == 0), stop=(c == 1))
                last.then_inc(L[1]["w_ps"], 1)

            def window_sum(s, k):
                eng.wait_ge(L[1]["msg"], after(s))
                eng.wait_ge(L[1]["oh"], after(s))
                eng.wait_ge(L[1]["added"], after(s - 1))
                for t in range(T):
                    last = nc.tensor.matmul(ps_a[0:D, 0:WIN], msg[:, k % 2, t, :], oh[:, k % 2, t, :],
                                            start=(t == 0), stop=(t == T - 1))
                last.then_inc(L[1]["acc"], 1)

            def program(fast):
                for name in ("oht_ps", "key_ps", "x_ps", "comb_ps"):
                    eng.sem_inc(L[0][name], PRIME)
                for name in ("hps0", "hps1", "w_ps", "acc", "key_ps", "comb_ps"):
                    eng.sem_inc(L[1][name], PRIME)
                for k in range(2):
                    if fast:
                        one_hot_turn(k, k)
                    keys(0, k, k)
                if fast:
                    pick(0, 0, 0)

                def step0(s, k, i, more):
                    if more(2):
                        keys(0, s + 2, k + 2)
                    if fast and more(1):
                        pick(s + 1, k + 1, i)
                    combine(0, s, k)
                    if fast and more(2):
                        one_hot_turn(s + 2, k + 2)
                sweep(eng, step0)
                eng.wait_ge(s_w1k, 1)
                eng.wait_ge(s_w2, 1)
                eng.wait_ge(s_normed[0], 1)
                hidden(0, 0, 0)
                hidden(1, 1, 0)
                weights(0, 0)

                def step1(s, k, i, more):
                    if more(2):
                        hidden(s + 2, k + 2, i)
                    if more(1):
                        weights(s + 1, k + 1)
                    if fast:
                        window_sum(s, k)
                    else:
                        keys(1, s, k)
                        combine(1, s, k)
                sweep(eng, step1)
                if fast:
                    eng.wait_ge(L[1]["added"], after(NSB - 1))
                    eng.wait_ge(L[1]["pv"], after(NSB - 1))
                    acc_v = big[0:D, 0:NP].rearrange("f (p j) -> f j p", j=NJ)
                    for j in range(NJ):
                        if j % 16 == 0 and j >= 64:
                            eng.wait_ge(s_turned_read, j // 16 - 3)
                        last = nc.tensor.transpose(ps_w[:, j // 16 % 4, j % 16 * D:(j % 16 + 1) * D],
                                                   acc_v[:, j, :], ident[0:D, 0:D])
                        if j % 16 == 15 or j == NJ - 1:
                            last.then_inc(s_turned, 1)
            both(eng, program)

        @block.vector
        def _(eng):
            V = nc.vector
            eng.wait_ge(s_edges, 48)
            rel_v = rel[:, :].rearrange("p (s t) -> p s t", t=T)
            V.tensor_tensor(rel_v, dst_i[:, :].rearrange("p (s t) -> p s t", t=T),
                            spread(first_i[:, :], 2, T), ALU.subtract).then_inc(s_step, 1)
            eng.wait_ge(s_step, 1)
            V.tensor_scalar(nrel[:, :], rel[:, :], -1.0, None, ALU.mult).then_inc(s_nrel, 1)
            V.tensor_reduce(ext[:, 0:1], rel[:, :], AX_X, ALU.max).then_inc(s_step, 1)
            V.tensor_reduce(ext[:, 1:2], rel[:, :], AX_X, ALU.min).then_inc(s_step, 1)
            eng.wait_ge(s_step, 3)
            V.tensor_scalar(ext[:, 2:3], ext[:, 0:1], WIN - 0.5, None, ALU.is_gt).then_inc(s_ext, 1)
            V.tensor_scalar(ext[:, 3:4], ext[:, 1:2], -0.5, None, ALU.is_lt).then_inc(s_ext, 1)
            eng.wait_ge(s_ext, 2)
            V.tensor_tensor(ext[:, 4:5], ext[:, 2:3], ext[:, 3:4], ALU.add).then_inc(s_step, 1)
            eng.wait_ge(s_flagps, 1)
            V.tensor_scalar(flag_i[:, :], ps_a[0:1, 0:1], 0.5, None, ALU.is_gt).then_inc(s_flag, 1)

            x_rows = [v.rearrange("p (r f) -> p r f", f=D) for v in (x_f, x_r)]
            eng.wait_ge(s_xa, 1)
            V.tensor_tensor(x_rows[1], x_rows[0], x_b[:, 0], ALU.subtract).then_inc(s_xr, 1)
            eng.wait_ge(s_xb, 1)
            V.tensor_tensor(x_b[:, 2], x_rows[1], x_b[:, 1], ALU.subtract).then_inc(s_xc, 1)

            eng.wait_ge(s_wload, 16 * 10)
            eng.wait_ge(s_const, 13)
            w = lambda j: w1s[:, j, :]
            chain = [0]

            def link(ins):
                chain[0] += 1
                ins.then_inc(s_link, 1)
                eng.wait_ge(s_link, chain[0])
            link(V.tensor_copy(w1p[:, 0, :], w(0)))
            link(V.tensor_tensor(w(1), w(0), w1p[:, 0, :], ALU.subtract))
            link(V.tensor_copy(w1p[:, 1, :], w(1)))
            link(V.tensor_tensor(w(2), w(1), w1p[:, 1, :], ALU.subtract))
            link(V.tensor_copy(w1p[:, 2, :], w(2)))
            link(V.tensor_scalar(w(3), w1p[:, 0, :], w1m[:, 0:1], None, ALU.mult))
            link(V.scalar_tensor_tensor(w(4), w1p[:, 1, :], w1m[:, 1:2], w(3), ALU.mult, ALU.add))
            V.scalar_tensor_tensor(w1k[:, :], w1p[:, 2, :], w1m[:, 2:3], w(4), ALU.mult, ALU.add)\
                .then_inc(s_w1k, 1)
            scale = (1.0 / HID ** 0.5) * (1.0 / 128.0) ** 0.5 / (E / N) ** 0.5
            link(V.tensor_scalar(w2s[:, :, :], w2s[:, :, :], scale, None, ALU.mult))
            V.tensor_scalar(w2s[:, :, 2 * MUL * MUL:3 * MUL * MUL], w2s[:, :, 2 * MUL * MUL:3 * MUL * MUL],
                            1.0 / 3.0 ** 0.5, None, ALU.mult).then_inc(s_w2, 1)

            def split(k, i):
                if k == 2:
                    eng.wait_ge(s_esa, i + 1)
                    V.tensor_tensor(es_r, es_f, es_b[0][:, :], ALU.subtract).then_inc(s_esr, 1)
                if k == 4:
                    eng.wait_ge(s_esb, i + 1)
                    V.tensor_tensor(es_b[2][:, :], es_r, es_b[1][:, :], ALU.subtract).then_inc(s_esc, 1)

            def key_cast(n, s, k, ids):
                eng.wait_ge(L[n]["sidx"], after(s - 2))
                V.tensor_copy(keyf[:, k % 2, :], ids[:, bass.ds(s * T, T)]).then_inc(L[n]["keyf"], 1)

            def one_hot(s, k):
                eng.wait_ge(L[0]["oht_ps"], after(s - 2))
                V.tensor_tensor(oh_b[:, k % 2, :, :], spread(iota_ps, 1, T),
                                spread(rel[:, bass.ds(s * T, T)], 2, WIN), ALU.is_equal)\
                    .then_inc(L[0]["oh"], 1)

            def dedupe(n, s, k):
                b = k % 2
                key_ps = key_ps0 if n == 0 else key_ps1
                eng.wait_ge(L[n]["keyf"], after(s))
                eng.wait_ge(L[n]["key_ps"], after(s))
                eng.wait_ge(L[n]["comb"], after(s - SLOTS))
                V.tensor_tensor(same[:, k % SLOTS, :, :], key_ps, spread(keyf[:, b, :], 2, P), ALU.is_equal)\
                    .then_inc(L[n]["same"], 1)
                for t in range(T):
                    last = V.scalar_tensor_tensor(junk[:, t, :], key_ps[:, t, :], keyf[:, b, t:t + 1], tri[:, :],
                                                  ALU.is_equal, ALU.mult, accum_out=dup[:, b, 0, t:t + 1])
                last.then_inc(L[n]["key_free"], 1)
                V.tensor_scalar(dup[:, b, 1, :], keyf[:, b, :], -1.0, trash[:, :], ALU.mult, ALU.add)\
                    .then_inc(L[n]["scaled"], 1)
                eng.wait_ge(L[n]["key_free"], after(s))
                eng.wait_ge(L[n]["scaled"], after(s * 2))
                V.scalar_tensor_tensor(dup[:, b, 2, :], dup[:, b, 0, :], 0.5, dup[:, b, 1, :],
                                       ALU.is_gt, ALU.mult).then_inc(L[n]["scaled"], 1)
                eng.wait_ge(L[n]["scaled"], after(s * 2 + 1))
                eng.wait_ge(L[n]["retired"], s * T + T)
                V.tensor_tensor(sidx[:, k % RING, :], dup[:, b, 2, :], keyf[:, b, :], ALU.add)\
                    .then_inc(L[n]["sidx"], 1)

            def message(s, k, i, fast):
                eng.wait_ge(L[0]["comb"], after(s - 2))
                if fast:
                    eng.wait_ge(L[0]["x_ps"], after(s))
                    rows = x_ps
                else:
                    eng.wait_ge(s_gat[0][k % SLOTS], uses(i, k) * 16 * T + 16 * T)
                    rows = gat[:, k % SLOTS, :, :]
                V.tensor_tensor(msg[:, k % 2, :, :], rows, spread(wgt[:, bass.ds(s * T, T)], 2, D), ALU.mult)\
                    .then_inc(L[0]["msg"], 1)

            def sh_at(s):
                return sh_sb[:, bass.ds(s * (4 * T), 4 * T)].rearrange("p (t c) -> p t c", t=T)

            def pre(s, k, i):
                q = k % SLOTS
                eng.wait_ge(s_gat[1][q], uses(i, k) * 16 * T + 16 * T)
                V.tensor_tensor(vv[:, :, :, :], gat[:, q, :, MUL:D].rearrange("p t (u i) -> p t u i", i=3),
                                spread(sh_at(s)[:, :, 1:4], 2, MUL), ALU.mult).then_inc(L[1]["pre"], 1)

            def tensor_product(s, k, between):
                q = k % SLOTS
                wv = ps_w[:, 2 * (k % 2):2 * (k % 2) + 2, :].rearrange("p b (t n) -> p (b t) n", t=2)
                m2 = MUL * MUL
                eng.wait_ge(L[1]["w_ps"], after(s))
                V.tensor_tensor(prod_s[:, :, :, :], wv[:, :, 0:2 * m2].rearrange("p t (u w) -> p t u w", u=MUL),
                                spread(gat[:, q, :, 0:MUL], 3, 2 * MUL), ALU.mult).then_inc(L[1]["ps"], 1)
                eng.wait_ge(L[1]["pre"], after(s))
                V.tensor_reduce(vdot[:, :, :], vv[:, :, :, :], AX_X, ALU.add).then_inc(L[1]["dot"], 1)
                vec = gat[:, q, :, MUL:D].rearrange("p t (u i) -> p t u i", i=3)
                for c in range(3):
                    V.tensor_tensor(prod_v[:, :, c, :, :],
                                    wv[:, :, 3 * m2:4 * m2].rearrange("p t (u w) -> p t u w", u=MUL),
                                    spread(vec[:, :, :, c], 3, MUL), ALU.mult)
                eng.wait_ge(L[1]["dot"], after(s))
                V.tensor_tensor(prod_v[:, :, 3, :, :], wv[:, :, 2 * m2:3 * m2].rearrange("p t (u w) -> p t u w", u=MUL),
                                spread(vdot[:, :, :], 3, MUL), ALU.mult).then_inc(L[1]["pv"], 1)
                eng.wait_ge(L[1]["ps"], after(s))
                V.tensor_reduce(red[:, :, 0:2, :].rearrange("p t c w -> p t (c w)"),
                                prod_s[:, :, :, :].rearrange("p t u n -> p t n u"), AX_X, ALU.add)\
                    .then_inc(L[1]["rs"], 1)
                eng.wait_ge(L[1]["pv"], after(s))
                V.tensor_reduce(red[:, :, 2:6, :], prod_v[:, :, :, :, :].rearrange("p t c u w -> p (t c) w u"),
                                AX_X, ALU.add).then_inc(L[1]["rv"], 1)
                add = between()
                eng.wait_ge(L[1]["rs"], after(s))
                V.tensor_tensor(red[:, :, 6:9, :], spread(red[:, :, 0, :], 2, 3),
                                spread(sh_at(s)[:, :, 1:4], 3, MUL), ALU.mult).then_inc(L[1]["cross"], 1)
                eng.wait_ge(L[1]["rv"], after(s))
                V.tensor_tensor(red[:, :, 1:5, :].rearrange("p t c w -> p t (c w)"),
                                red[:, :, 1:5, :].rearrange("p t c w -> p t (c w)"),
                                spread(sh_at(s)[:, :, 0], 2, 4 * MUL), ALU.mult).then_inc(L[1]["outer"], 1)
                add()
                eng.wait_ge(L[1]["cross"], after(s))
                eng.wait_ge(L[1]["outer"], after(s))
                V.tensor_tensor(msg[:, k % 2, :, :], red[:, :, 1:5, :].rearrange("p t c w -> p t (c w)"),
                                red[:, :, 5:9, :].rearrange("p t c w -> p t (c w)"), ALU.add)\
                    .then_inc(L[1]["msg"], 1)

            def add_window(s, k):
                base = eng.value_load(first_i[0:1, bass.ds(s, 1)], min_val=0, max_val=N - 1)

                def add():
                    eng.wait_ge(L[1]["acc"], after(s))
                    eng.wait_ge(L[1]["added"], after(s - 1))
                    V.tensor_tensor(big[0:D, bass.ds(base, WIN)], ps_a[0:D, 0:WIN], big[0:D, bass.ds(base, WIN)],
                                    ALU.add).then_inc(L[1]["added"], 1)
                return add

            def table_sum():
                for t in range(1, T):
                    V.tensor_tensor(work[:, :], big[:, 0:NJ * D] if t == 1 else work[:, :],
                                    big[:, t * NJ * D:(t + 1) * NJ * D], ALU.add).then_inc(s_link, 1)
                    chain[0] += 1
                    eng.wait_ge(s_link, chain[0])

            def norm(n, dest):
                zv = work[:, :].rearrange("p (j f) -> p j f", f=D)
                link(V.tensor_reduce(stat[:, 0, :], zv, AX_X, ALU.add))
                link(V.tensor_scalar(stat[:, 3, :], stat[:, 0, :], -1.0 / D, None, ALU.mult))
                V.tensor_tensor(zv, zv, spread(stat[:, 3, :], 2, D), ALU.add).then_inc(s_centred[n], 1)
                eng.wait_ge(s_squared[n], 1)
                V.tensor_reduce(stat[:, 1, :], big[:, 0:NJ * D].rearrange("p (j f) -> p j f", f=D),
                                AX_X, ALU.add).then_inc(s_summed[n], 1)
                eng.wait_ge(s_std[n], 1)
                link(V.reciprocal(stat[:, 3, :], stat[:, 2, :]))
                V.tensor_tensor(dest[:, :].rearrange("p (j f) -> p j f", f=D), zv,
                                spread(stat[:, 3, :], 2, D), ALU.mult).then_inc(s_normed[n], 1)

            def program(fast):
                saved = chain[0]
                for name in ("keyf", "oh", "same", "key_free", "scaled", "sidx", "msg"):
                    eng.sem_inc(L[0][name], PRIME)
                for name in ("keyf", "same", "key_free", "scaled", "sidx", "msg", "pre", "dot", "ps",
                             "pv", "rs", "rv", "cross", "outer", "added"):
                    eng.sem_inc(L[1][name], PRIME)
                eng.wait_ge(s_iotab, 1)
                eng.wait_ge(s_w, 16)
                def prepare(s, k):
                    key_cast(0, s, k, src_i)
                    if fast:
                        one_hot(s, k)

                for k in range(2):
                    prepare(k, k)
                    dedupe(0, k, k)
                message(0, 0, 0, fast)
                prepare(2, 2)

                def step0(s, k, i, more):
                    if more(3):
                        prepare(s + 3, k + 3)
                    if more(1):
                        message(s + 1, k + 1, i, fast)
                    if more(2):
                        dedupe(0, s + 2, k + 2)
                    split(k, i)
                sweep(eng, step0)
                eng.wait_ge(s_tab, 16 * T)
                table_sum()
                norm(0, x1)
                if fast:
                    link(V.memset(big[0:D, :], 0.0))
                eng.wait_ge(s_sh, 16)

                def step1(s, k, i, more, head=False):
                    if not fast:
                        key_cast(1, s, k, dst_i)
                        dedupe(1, s, k)
                    pre(s, k, i)
                    first_s = isinstance(s, int) and s == 0
                    tensor_product(s, k, lambda: add_window(s - 1, k) if fast and not first_s else lambda: None)
                sweep(eng, step1, head=1)
                if fast:
                    add_window(NSB - 1, U - 1)()
                if fast:
                    for g in range(-(-NJ // 16)):
                        eng.wait_ge(s_turned, g + 1)
                        j0, j1 = 16 * g, min(NJ, 16 * g + 16)
                        part = ps_w[:, g % 4, 0:(j1 - j0) * D].rearrange("p (j f) -> p j f", f=D)
                        last = add_nodes(j0, j1, part)
                        last.then_inc(s_turned_read, 1)
                    eng.wait_ge(s_turned_read, -(-NJ // 16))
                else:
                    eng.wait_ge(s_tab, 32 * T)
                    table_sum()
                    link(V.tensor_copy(big[:, 0:NJ * D], work[:, :]))
                    link(add_nodes(0, NJ, big[:, 0:NJ * D].rearrange("p (j f) -> p j f", f=D)))
                norm(1, work)
                chain[0] = saved

            def add_nodes(j0, j1, part):
                xv = x1[:, j0 * D:j1 * D].rearrange("p (j f) -> p j f", f=D)
                wv = work[:, j0 * D:j1 * D].rearrange("p (j f) -> p j f", f=D)
                V.tensor_tensor(wv[:, :, 0:MUL], xv[:, :, 0:MUL], part[:, :, 0:MUL], ALU.add)
                return V.tensor_tensor(wv[:, :, MUL:D].rearrange("p j (w i) -> p j w i", i=3),
                                       xv[:, :, MUL:D].rearrange("p j (w i) -> p j w i", i=3),
                                       part[:, :, MUL:D].rearrange("p j (i w) -> p j w i", i=3), ALU.add)
            both(eng, program)




def kernel(x, src, dst, edge_attr_4, edge_attr_8, edge_weight, L1_gnn_fc_w1, L1_gnn_fc_w2):
    import numpy as np
    import concourse.bacc as bacc
    from concourse.bass_utils import run_bass_kernel_spmd

    def edges(a, how="constant"):
        a = np.pad(np.asarray(a), [(0, EP - E)] + [(0, 0)] * (a.ndim - 1), mode=how)
        return a.reshape(NSB, P, T, -1)

    def on_partitions(a):
        return np.ascontiguousarray(a.transpose(1, 0, 2, 3).reshape(P, -1))

    targets = edges(dst, "edge")
    w2 = np.asarray(L1_gnn_fc_w2).reshape(HID, 4, MUL, MUL)
    w2 = np.concatenate([w2[:, 2::-2].transpose(0, 2, 1, 3).reshape(HID, -1),
                         w2[:, 1].reshape(HID, -1), w2[:, 3].reshape(HID, -1)], axis=1)
    arrays = {
        "x": np.pad(np.asarray(x), [(0, ROWS - N), (0, 0)]),
        "src": on_partitions(edges(src)),
        "dst": on_partitions(targets),
        "first": np.ascontiguousarray(np.broadcast_to(targets[:, 0, 0, 0], (P, NSB))),
        "weight": on_partitions(edges(edge_weight)),
        "sh": on_partitions(edges(edge_attr_4)),
        "es": np.ascontiguousarray(edges(edge_attr_8).transpose(3, 0, 2, 1).reshape(BASIS, EP)),
        "w1": np.ascontiguousarray(L1_gnn_fc_w1),
        "w2": np.ascontiguousarray(w2),
    }
    nc = bacc.Bacc("TRN2", target_bir_lowering=False, num_devices=1)
    args = [nc.dram_tensor(name, a.shape, mybir.dt.from_np(a.dtype), kind="ExternalInput").ap()
            for name, a in arrays.items()]
    out = nc.dram_tensor("out", (NP, D), F32, kind="ExternalOutput").ap()
    gnn_kernel(nc, *args, out)
    r = run_bass_kernel_spmd(nc, [arrays], core_ids=[0])
    return r.results[0]["out"][0:N]
```

```python
from contextlib import ExitStack

import concourse.bass as bass
from concourse import mybir

F32 = mybir.dt.float32
BF16 = mybir.dt.bfloat16
I32 = mybir.dt.int32
ALU = mybir.AluOpType
ACT = mybir.ActivationFunctionType
AX_X = mybir.AxisListType.X

P = 128
N, E, D = 12500, 200000, 32
MUL, BASIS, HID = 8, 8, 256
T = 4
SB = P * T
U = 8
TURNS = -(-E // (SB * U))
NSB = TURNS * U
EP = NSB * SB
NJ = -(-N // P)
NP = P * NJ
ROWS = NP + P
WIN = P
SLOTS = 4
RING = 8
PRIME = 6
EPS = 1e-5
ESCOLS = 8 * EP // P
ESPART = ESCOLS // TURNS
NSPLIT = 3
KROWS = NSPLIT * NSPLIT * BASIS
CROSS = 5
CONSTS = 14 + T
PARTS = 7
PJ = NJ // PARTS
XPARTS = 3
CHUNK = 4


def after(s):
    return s + (1 + PRIME)


def spread(ap, axis, count):
    ap = ap.unsqueeze(axis)
    shape = list(ap.shape)
    shape[axis] = count
    return ap.to_broadcast(shape)


def gnn_kernel(nc, x, src, dst, first, weight, sh, es, w1, w2, out):
    tables = [nc.dram_tensor(f"table{t}", [ROWS, D], F32, kind="Internal").ap() for t in range(T)]
    nodes1 = nc.dram_tensor("nodes1", [NP, D], F32, kind="Internal").ap()
    x_split = nc.dram_tensor("x_split", [ROWS, NSPLIT * D], BF16, kind="Internal").ap()
    es_split = nc.dram_tensor("es_split", [NSPLIT * BASIS, EP], BF16, kind="Internal").ap()

    ctx = ExitStack()
    with ctx:
        def sb(name, shape, dt=F32):
            return ctx.enter_context(nc.sbuf_tensor(name, shape, dt))

        def sem(name):
            return ctx.enter_context(nc.semaphore(name))

        src_i = sb("src_i", [P, NSB * T], I32)
        dst_i = sb("dst_i", [P, NSB * T], I32)
        first_i = sb("first_i", [P, NSB], I32)
        rel = sb("rel", [P, NSB * T])
        nrel = sb("nrel", [P, NSB * T])
        wgt = sb("wgt", [P, NSB * T])
        sh_sb = sb("sh_sb", [P, NSB * T * 4])
        big = sb("big", [P, ROWS])
        x1 = sb("x1", [P, NJ * D])
        work = sb("work", [P, NJ * D])
        stat = sb("stat", [P, 4, NJ])
        iota_sb = sb("iota_sb", [P, P])
        tri = sb("tri", [P, P])
        ident = sb("ident", [P, P])
        stack = sb("stack", [P, D])
        identb = sb("identb", [P, P], BF16)
        onescol = sb("onescol", [P, 1])
        zeros = sb("zeros", [P, ROWS // P * D // 3])
        trash = sb("trash", [P, 1])
        eps = sb("eps", [P, 1])
        ext = sb("ext", [P, 8])
        flag_i = sb("flag_i", [1, 1], I32)
        w1s = sb("w1s", [KROWS, 6, HID])
        w1p = sb("w1p", [KROWS, NSPLIT, HID], BF16)
        w1m = sb("w1m", [KROWS, NSPLIT])
        w1k = sb("w1k", [KROWS, HID], BF16)
        w2s = sb("w2s", [P, 2, HID])
        keyf = sb("keyf", [P, 2, T])
        oh_b = sb("oh_b", [P, 2, T, WIN], BF16)
        oht = sb("oht", [P, 2, T, P], BF16)
        oh = sb("oh", [P, 2, T, WIN])
        same = sb("same", [P, SLOTS, T, P])
        junk = sb("junk", [P, T, P])
        sq = junk
        dup = sb("dup", [P, 2, 3, T])
        xwin = sb("xwin", [P, SLOTS, NSPLIT * D], BF16)
        msg = sb("msg", [P, 2, T, D])
        comb = sb("comb", [P, RING, T, D])
        sidx = sb("sidx", [P, RING, T], I32)
        gidx = sb("gidx", [P, SLOTS, T], I32)
        gat = sb("gat", [P, SLOTS, T, D])
        hs = sb("hs", [KROWS, 2, CHUNK * SB], BF16)
        hT = sb("hT", [P, 2, 2, SB])
        vv = sb("vv", [P, 2 * T, MUL, 3])
        vdot = sb("vdot", [P, T, MUL])
        coef = sb("coef", [P, 2, T * MUL, 6])
        prod = sb("prod", [P, T * MUL, 6, MUL])
        red = sb("red", [P, 2 * T, 2 + 3 * CROSS, MUL])

        es_sb = sb("es_sb", [P, 2 * ESPART])
        es_b = [sb(f"es_b{m}", [P, ESPART], BF16) for m in range(NSPLIT)]

        ps_w = ctx.enter_context(nc.psum_tensor("ps_w", [P, 4, 512], F32))
        ps_h = ctx.enter_context(nc.psum_tensor("ps_h", [P, 2, 512], F32))
        ps_d = ctx.enter_context(nc.psum_tensor("ps_d", [P, 512], F32))
        ps_a = ctx.enter_context(nc.psum_tensor("ps_a", [P, 512], F32))
        XC = ROWS // P * D
        x_f, x_r = big[:, 0:XC], big[:, XC:2 * XC]
        x_parts = big[:, 2 * XC:2 * XC + NSPLIT * XC // 2].bitcast(BF16)
        x_b = x_parts.rearrange("p (r m f) -> p m r f", m=NSPLIT, f=D)
        XR = ROWS // P // XPARTS
        es_f = es_sb[:, 0:ESPART]
        es_r = es_sb[:, ESPART:2 * ESPART]
        iota_ps = ps_d[:, 0:P]
        oht_ps = ps_w[:, 0, 0:SB // 2].bitcast(BF16).rearrange("p (t e) -> p t e", t=T)
        x_ps = ps_w[:, 1, 0:T * D].rearrange("p (t f) -> p t f", t=T)
        key_ps0 = ps_w[:, 2, :].rearrange("p (t e) -> p t e", t=T)
        comb_ps0 = ps_w[:, 3, 0:T * D].rearrange("p (t f) -> p t f", t=T)
        key_ps1 = ps_d[:, :].rearrange("p (t e) -> p t e", t=T)
        comb_ps1 = ps_a[:, 0:T * D].rearrange("p (t f) -> p t f", t=T)

        ps_acc = (ps_a, ps_d)

        s_edges, s_w, s_sh, s_wload = map(sem, ("s_edges", "s_w", "s_sh", "s_wload"))
        s_init = [sem(f"s_init{t}") for t in range(T)]
        s_const, s_iotab, s_zero, s_step, s_flag, s_flagps = map(
            sem, ("s_const", "s_iotab", "s_zero", "s_step", "s_flag", "s_flagps"))
        s_xin = [sem(f"s_xin{h}") for h in range(XPARTS)]
        s_xa, s_xr, s_xb, s_xc, s_xsplit = map(sem, ("s_xa", "s_xr", "s_xb", "s_xc", "s_xsplit"))
        s_nrel, s_esdone = sem("s_nrel"), sem("s_esdone")
        s_w1k, s_w2, s_link, s_ext = sem("s_w1k"), sem("s_w2"), sem("s_link"), sem("s_ext")
        s_es, s_esa, s_esb, s_esr, s_esc, s_esout = map(
            sem, ("s_es", "s_esa", "s_esb", "s_esr", "s_esc", "s_esout"))
        s_tab = [sem(f"s_tab{c}") for c in range(PARTS)]
        s_cleared = sem("s_cleared")
        s_x1out, s_out = sem("s_x1out"), sem("s_out")
        s_turned, s_turned_read = sem("s_turned"), sem("s_turned_read")
        s_landed = [sem(f"s_landed{n}") for n in range(2)]
        s_two, s_other, s_joined, s_rowsum, s_mean, s_centred, s_squared, s_summed, s_std, s_recip, s_normed = map(
            sem, ("s_two", "s_other", "s_joined", "s_rowsum", "s_mean", "s_centred", "s_squared", "s_summed",
                  "s_std", "s_recip", "s_normed"))

        def layer_sems(n):
            return {name: sem(f"{name}{n}") for name in (
                "keyf", "oh", "oht_ps", "oht", "key_ps", "same", "key_free", "sidx", "x_ps",
                "msg", "comb_ps", "comb", "retired", "gidx", "hps0", "hps1", "ht0", "ht1",
                "w_ps", "pre", "dot", "coef", "pv", "rv", "scaled",
                "cross", "sq", "asked", "acc", "added")}
        L = [layer_sems(0), layer_sems(1)]
        s_xwin = [sem(f"s_xwin{q}") for q in range(SLOTS)]
        s_gat = [[sem(f"s_gat{n}_{q}") for q in range(SLOTS)] for n in range(2)]
        s_scat = [[sem(f"s_scat{n}_{t}") for t in range(T)] for n in range(2)]
        s_hs = [sem(f"s_hs{b}") for b in range(2)]

        block = ctx.enter_context(nc.Block())

        def sweep(eng, step, head=0):
            for i in range(head):
                for k in range(U):
                    step(i * U + k, k, i, lambda d: True)
            with eng.Fori(head, TURNS - 1) as i:
                for k in range(U):
                    step(i * U + k, k, i, lambda d: True)
            for k in range(U):
                step((TURNS - 1) * U + k, k, TURNS - 1, lambda d: k + d < U)

        def uses(i, k):
            return i * (U // SLOTS) + k // SLOTS

        def part(c, table=0):
            return slice((table * NJ + c * PJ) * D, (table * NJ + (c + 1) * PJ) * D)

        def squares(c):
            return prod[:, :, :, :].rearrange("p g c w -> p (g c w)")[:, c % 3 * PJ * D:(c % 3 + 1) * PJ * D]

        def part_rows(t, c):
            return t[0:NP, :].rearrange("(p r) f -> p (r f)", p=P)[:, part(c)]

        def both(eng, program):
            eng.wait_ge(s_flag, 1)
            flag = eng.value_load(flag_i[0:1, 0:1], min_val=0, max_val=1)
            with eng.If(flag == 0):
                program(True)
            with eng.Else():
                program(False)

        @block.sync
        def _(eng):
            for h in range(XPARTS):
                cols = slice(h * XR * D, (h + 1) * XR * D)
                eng.dma_start(x_f[:, cols], x.rearrange("(p r) f -> p (r f)", p=P)[:, cols]).then_inc(s_xin[h], 16)
            eng.dma_start(dst_i[:, :], dst).then_inc(s_edges, 16)
            eng.dma_start(first_i[:, :], first).then_inc(s_edges, 16)
            eng.dma_start(src_i[:, :], src).then_inc(s_edges, 16)
            eng.dma_start(wgt[:, :], weight).then_inc(s_w, 16)
            for q in range(NSPLIT * NSPLIT):
                eng.dma_start(w1s[q * BASIS:(q + 1) * BASIS, 0, :], w1).then_inc(s_wload, 16)
            eng.dma_start(w2s[:, :, :], w2.rearrange("(c p) n -> p c n", c=2)).then_inc(s_wload, 16)
            for h in range(XPARTS):
                cols = slice(h * XR * NSPLIT * D, (h + 1) * XR * NSPLIT * D)
                eng.wait_ge(s_xc, h + 1)
                eng.dma_start(x_split.rearrange("(p r) f -> p (r f)", p=P)[:, cols], x_parts[:, cols])\
                    .then_inc(s_xsplit, 16)

            def zero_table(t):
                eng.dma_start(tables[t].rearrange("(p a r) f -> p a (r f)", p=P, a=3),
                              spread(zeros[:, :], 1, 3)).then_inc(s_init[t], 16)

            eng.dma_start(tables[0].rearrange("(p r) f -> p (r f)", p=P),
                          x.rearrange("(p r) f -> p (r f)", p=P)).then_inc(s_init[0], 16)
            eng.wait_ge(s_zero, 1)
            zero_table(1)

            es_out = es_split.rearrange("(m r) (c n) -> m (r c) n", m=NSPLIT, c=P // BASIS)
            es_in = es.rearrange("r (c n) -> (r c) n", c=P // BASIS)

            def split_io(k, i):
                if k == 0:
                    eng.wait_ge(s_esdone, i * 2 + 1)
                    eng.dma_start(es_f, es_in[:, bass.ds(i * ESPART, ESPART)]).then_inc(s_es, 16)
                if k == U - 1:
                    eng.wait_ge(s_esc, i + 1)
                    eng.sem_inc(s_esdone, 1)
                    for m in range(NSPLIT):
                        eng.dma_start(es_out[m, :, bass.ds(i * ESPART, ESPART)], es_b[m][:, :]).then_inc(s_esout, 16)
                    eng.wait_ge(s_esout, i * (16 * NSPLIT) + 16 * NSPLIT)
                    eng.sem_inc(s_esdone, 1)

            def load_tables():
                for c in range(PARTS):
                    for t in range(T):
                        eng.dma_start(big[:, part(c, t)], part_rows(tables[t], c)).then_inc(s_tab[c], 16)

            def program(fast):
                def window(s, k, i, more):
                    if fast:
                        base = eng.value_load(first_i[0:1, bass.ds(s, 1)], min_val=0, max_val=N - 1)
                        eng.wait_ge(L[0]["x_ps"], after(s - SLOTS))
                        eng.dma_start(xwin[:, k % SLOTS, :], x_split[bass.ds(base, WIN), :]).then_inc(s_xwin[k % SLOTS], 16)
                    if isinstance(s, int) and s == SLOTS - 1:
                        for t in range(2, T):
                            zero_table(t)
                    if isinstance(s, int) and s >= U:
                        cols = slice(k * NSB * T * 4 // U, (k + 1) * NSB * T * 4 // U)
                        eng.dma_start(sh_sb[:, cols], sh[:, cols]).then_inc(s_sh, 16)
                    split_io(k, i)
                eng.wait_ge(s_edges, 48)
                eng.wait_ge(s_xsplit, 16 * XPARTS)
                eng.sem_inc(s_esdone, 1)
                sweep(eng, window, head=1)
                eng.wait_ge(s_landed[0], 1)
                load_tables()
                for c in range(PARTS):
                    eng.wait_ge(s_normed, c + 1)
                    eng.dma_start(part_rows(nodes1, c), x1[:, part(c)]).then_inc(s_x1out, 16)
                if not fast:
                    for c in range(PARTS):
                        eng.wait_ge(s_tab[c], 16 * T)
                    for t in range(T):
                        zero_table(t)

                def scalars(s, k, i, more):
                    if k % CHUNK:
                        return
                    eng.wait_ge(L[1]["hps1"], after(s - CHUNK - 1))
                    b = k // CHUNK
                    for m in range(NSPLIT):
                        eng.dma_start(hs[m * NSPLIT * BASIS:(m + 1) * NSPLIT * BASIS, b, :],
                                      es_split[:, bass.ds(s * SB, CHUNK * SB)]).then_inc(s_hs[b], 16)
                sweep(eng, scalars)
                if not fast:
                    eng.wait_ge(s_landed[1], 1)
                    load_tables()
                for c in range(PARTS):
                    eng.wait_ge(s_normed, PARTS + c + 1)
                    eng.dma_start(part_rows(out, c), work[:, part(c)]).then_inc(s_out, 16)
                eng.wait_ge(s_x1out, 16 * PARTS)
                eng.wait_ge(s_out, 16 * PARTS)
            both(eng, program)

        @block.gpsimd
        def _(eng):
            nc.gpsimd.memset(zeros[:, :], 0.0).then_inc(s_zero, 1)
            nc.gpsimd.iota(iota_sb[:, :], pattern=[[1, P]], base=0, channel_multiplier=0,
                           allow_small_or_imprecise_dtypes=True).then_inc(s_const, 1)
            nc.gpsimd.iota(trash[:, :], pattern=[[0, 1]], base=NP, channel_multiplier=1,
                           allow_small_or_imprecise_dtypes=True).then_inc(s_const, 1)
            nc.gpsimd.memset(eps[:, :], EPS).then_inc(s_const, 1)
            nc.gpsimd.memset(onescol[:, :], 1.0).then_inc(s_const, 1)
            nc.gpsimd.memset(tri[:, :], 1.0).then_inc(s_const, 1)
            nc.gpsimd.memset(ident[:, :], 0.0).then_inc(s_const, 1)
            nc.gpsimd.memset(identb[:, :], 0.0).then_inc(s_const, 1)
            nc.gpsimd.memset(w1m[:, :], 1.0).then_inc(s_const, 1)
            nc.gpsimd.memset(stack[:, :], 0.0).then_inc(s_const, 1)
            eng.wait_ge(s_const, 9)
            nc.gpsimd.affine_select(out=tri[:, :], in_=tri[:, :], compare_op=ALU.is_gt, fill=0.0,
                                    base=0, pattern=[[-1, P]], channel_multiplier=1).then_inc(s_const, 1)
            for m in (ident, identb):
                nc.gpsimd.affine_select(out=m[:, :], in_=m[:, :], compare_op=ALU.not_equal, fill=1.0,
                                        base=0, pattern=[[-1, P]], channel_multiplier=1).then_inc(s_const, 1)
            nc.gpsimd.affine_select(out=w1m[:, :], in_=w1m[:, :], compare_op=ALU.is_ge, fill=0.0,
                                    base=0, pattern=[[-NSPLIT * BASIS, NSPLIT]],
                                    channel_multiplier=1).then_inc(s_const, 1)
            eng.wait_ge(s_const, 13)
            nc.gpsimd.affine_select(out=w1m[:, :], in_=w1m[:, :], compare_op=ALU.is_ge, fill=0.0,
                                    base=NSPLIT * BASIS - 1, pattern=[[NSPLIT * BASIS, NSPLIT]],
                                    channel_multiplier=-1).then_inc(s_const, 1)
            for t in range(T):
                eng.wait_ge(s_const, 14 + t)
                nc.gpsimd.affine_select(out=stack[:, :], in_=stack[:, :], compare_op=ALU.not_equal, fill=1.0,
                                        base=-t * D, pattern=[[-1, D]], channel_multiplier=1).then_inc(s_const, 1)

            def gather(n, s, k, i, table):
                q = k % SLOTS
                eng.wait_ge(L[n]["gidx"], after(s))
                eng.wait_ge(L[n]["msg" if n == 0 else "pv"], after(s - SLOTS))
                eng.sem_inc(L[n]["asked"], 1)
                for t in range(T):
                    nc.gpsimd.indirect_dma_start(
                        out=gat[:, q, t, :], out_offset=None, in_=table,
                        in_offset=bass.IndirectOffsetOnAxis(ap=gidx[:, q, t:t + 1], axis=0),
                    ).then_inc(s_gat[n][q], 16)

            def add_tables(n, clear):
                if clear:
                    nc.gpsimd.memset(big[:, T * NJ * D:], 0.0).then_inc(s_cleared, 1)
                for c in range(PARTS + 1):
                    if c < PARTS:
                        eng.wait_ge(s_tab[c], 16 * T * (n + 1))
                        nc.gpsimd.tensor_tensor(big[:, part(c, 2)], big[:, part(c, 2)], big[:, part(c, 3)], ALU.add)\
                            .then_inc(s_other, 1)
                    if c > 0 and clear:
                        eng.wait_ge(s_joined, c)
                        nc.gpsimd.memset(big[:, 0:T * NJ * D].rearrange("p (t n) -> p t n", t=T)[:, :, part(c - 1)],
                                         0.0).then_inc(s_cleared, 1)

            def first_one(s):
                return isinstance(s, int) and s == 0

            def scatter(n, s, k, head):
                q = k % RING
                eng.wait_ge(L[n]["comb"], after(s))
                eng.wait_ge(L[n]["sidx"], after(s))
                for t in range(T):
                    if head:
                        eng.wait_ge(s_init[t], 16 * (n + 1))
                    else:
                        eng.wait_ge(s_scat[n][t], s * 16)
                    eng.sem_inc(L[n]["retired"], 1)
                    nc.gpsimd.indirect_dma_start(
                        out=tables[t], out_offset=bass.IndirectOffsetOnAxis(ap=sidx[:, q, t:t + 1], axis=0),
                        in_=comb[:, q, t, :], in_offset=None, compute_op=ALU.add,
                    ).then_inc(s_scat[n][t], 16)

            def program(fast):
                eng.sem_inc(L[0]["retired"], (RING - 1) * T)
                if fast:
                    sweep(eng, lambda s, k, i, more: scatter(0, s, k, first_one(s)), head=1)
                else:
                    for k in range(2):
                        gather(0, k, k, 0, x)

                    def step(s, k, i, more):
                        if more(2):
                            gather(0, s + 2, k + 2, i, x)
                        scatter(0, s, k, first_one(s))
                    sweep(eng, step, head=1)
                for t in range(T):
                    eng.wait_ge(s_scat[0][t], NSB * 16)
                eng.sem_inc(s_landed[0], 1)
                add_tables(0, fast)
                eng.wait_ge(s_x1out, 16 * PARTS)
                if fast:
                    sweep(eng, lambda s, k, i, more: gather(1, s, k, i, nodes1))
                else:
                    eng.sem_inc(L[1]["retired"], (RING - 1) * T)
                    for k in range(3):
                        gather(1, k, k, 0, nodes1)

                    def step(s, k, i, more):
                        if more(3):
                            gather(1, s + 3, k + 3, i, nodes1)
                        scatter(1, s, k, first_one(s))
                    sweep(eng, step, head=1)
                    for t in range(T):
                        eng.wait_ge(s_scat[1][t], NSB * 16)
                    eng.sem_inc(s_landed[1], 1)
                    add_tables(1, False)
            both(eng, program)

        @block.scalar
        def _(eng):
            eng.wait_ge(s_const, CONSTS)
            nc.scalar.activation(iota_ps, iota_sb[:, :], ACT.Copy).then_inc(s_iotab, 1)
            x_rows = [v.rearrange("p (r f) -> p r f", f=D) for v in (x_f, x_r)]
            for h in range(XPARTS + 1):
                if h < XPARTS:
                    rows = slice(h * XR, (h + 1) * XR)
                    eng.wait_ge(s_xin[h], 16)
                    nc.scalar.activation(x_b[:, 0, rows], x_rows[0][:, rows], ACT.Copy).then_inc(s_xa, 1)
                if h > 0:
                    rows = slice((h - 1) * XR, h * XR)
                    eng.wait_ge(s_xr, h)
                    nc.scalar.activation(x_b[:, 1, rows], x_rows[1][:, rows], ACT.Copy).then_inc(s_xb, 1)

            def split(k, i):
                if k == 1:
                    eng.wait_ge(s_es, i * 16 + 16)
                    nc.scalar.activation(es_b[0][:, :], es_f, ACT.Copy).then_inc(s_esa, 1)
                if k == 3:
                    eng.wait_ge(s_esr, i + 1)
                    nc.scalar.activation(es_b[1][:, :], es_r, ACT.Copy).then_inc(s_esb, 1)

            def index(n, s, k, i, ids):
                eng.wait_ge(L[n]["msg" if n == 0 else "pv"], after(s - SLOTS))
                nc.scalar.activation(gidx[:, k % SLOTS, :], ids[:, bass.ds(s * T, T)], ACT.Copy)\
                    .then_inc(L[n]["gidx"], 1)

            def one_hot_out(s, k):
                eng.wait_ge(L[0]["oht_ps"], after(s))
                eng.wait_ge(L[0]["x_ps"], after(s - 2))
                nc.scalar.activation(oht[:, k % 2, :, :], oht_ps, ACT.Copy).then_inc(L[0]["oht"], 1)

            def comb_out(n, s, k):
                eng.wait_ge(L[n]["comb_ps"], after(s))
                eng.wait_ge(L[n]["retired"], s * T + T)
                nc.scalar.activation(comb[:, k % RING, :, :], comb_ps0 if n == 0 else comb_ps1, ACT.Copy)\
                    .then_inc(L[n]["comb"], 1)

            def hidden(s, k):
                for c in range(2):
                    eng.wait_ge(L[1][f"hps{c}"], after(s))
                    nc.scalar.activation(hT[:, k % 2, c, :], ps_h[:, c, :], ACT.Relu,
                                         scale=(2.0 / BASIS) ** 0.5).then_inc(L[1][f"ht{c}"], 1)

            def coefficients(s, k, i):
                q = k % SLOTS
                eng.wait_ge(s_gat[1][q], uses(i, k) * 16 * T + 16 * T)
                eng.wait_ge(L[1]["pv"], after(s - 2))
                nc.scalar.activation(coef[:, k % 2, :, 0],
                                     gat[:, q, :, :].rearrange("p t (u c) -> p (t u) c", c=4)[:, :, 0], ACT.Copy)
                for t in range(T):
                    last = nc.scalar.activation(coef[:, k % 2, t * MUL:(t + 1) * MUL, 2:6],
                                                gat[:, q, t, :].rearrange("p (u c) -> p u c", c=4), ACT.Identity,
                                                scale=sh_sb[:, bass.ds(s * (4 * T) + 4 * t, 1)])
                last.then_inc(L[1]["coef"], 1)

            def one_hot(s, k):
                eng.wait_ge(L[1]["oh"], after(s - 1))
                for t in range(T):
                    last = nc.scalar.activation(sq[:, t, :], iota_sb[:, :], ACT.Square,
                                                bias=nrel[:, bass.ds(s * T + t, 1)])
                last.then_inc(L[1]["sq"], 1)
                eng.wait_ge(L[1]["sq"], after(s))
                eng.wait_ge(L[1]["acc"], after(s - 2))
                nc.scalar.activation(oh[:, k % 2, :, :], sq[:, :, :], ACT.Relu, scale=-1.0, bias=onescol[:, :])\
                    .then_inc(L[1]["oh"], 1)

            def norm(n):
                for c in range(PARTS + 1):
                    if c > 0:
                        cols = slice((c - 1) * PJ, c * PJ)
                        eng.wait_ge(s_summed, n * PARTS + c)
                        nc.scalar.activation(stat[:, 2, cols], stat[:, 1, cols], ACT.Sqrt, bias=eps[:, :],
                                             scale=1.0 / D).then_inc(s_std, 1)
                    if c < PARTS:
                        eng.wait_ge(s_centred, n * PARTS + c + 1)
                        nc.scalar.activation(squares(c), work[:, part(c)], ACT.Square).then_inc(s_squared, 1)

            def program(fast):
                eng.sem_inc(L[0]["comb"], PRIME)
                eng.sem_inc(L[0]["oht"], PRIME)
                eng.sem_inc(L[0]["gidx"], PRIME)
                eng.sem_inc(L[1]["gidx"], PRIME)
                eng.wait_ge(s_nrel, 1)
                eng.sem_inc(L[1]["comb"], PRIME)
                eng.sem_inc(L[1]["ht0"], PRIME)
                eng.sem_inc(L[1]["ht1"], PRIME)
                eng.sem_inc(L[1]["sq"], PRIME)
                eng.sem_inc(L[1]["coef"], PRIME)
                eng.sem_inc(L[1]["oh"], PRIME)
                eng.wait_ge(s_edges, 48)
                if fast:
                    one_hot_out(0, 0)
                    one_hot_out(1, 1)
                else:
                    for k in range(3):
                        index(0, k, k, 0, dst_i)

                def step0(s, k, i, more):
                    if not fast and more(3):
                        index(0, s + 3, k + 3, i, dst_i)
                    if fast and more(2):
                        one_hot_out(s + 2, k + 2)
                    comb_out(0, s, k)
                    split(k, i)
                sweep(eng, step0)
                norm(0)
                for k in range(3):
                    index(1, k, k, 0, src_i)
                for k in range(2):
                    hidden(k, k)
                eng.wait_ge(s_sh, 16 * U)
                coefficients(0, 0, 0)

                def step1(s, k, i, more):
                    if more(3):
                        index(1, s + 3, k + 3, i, src_i)
                    if more(2):
                        hidden(s + 2, k + 2)
                    if more(1):
                        coefficients(s + 1, k + 1, i)
                    if fast and (not isinstance(s, int) or s >= 1):
                        one_hot(s - 1, k - 1)
                    if not fast and (not isinstance(s, int) or s >= 2):
                        comb_out(1, s - 2, k - 2)
                sweep(eng, step1, head=1)
                if fast:
                    one_hot(NSB - 1, U - 1)
                else:
                    for d in (2, 1):
                        comb_out(1, NSB - d, U - d)
                norm(1)
            both(eng, program)

        @block.tensor
        def _(eng):
            eng.wait_ge(s_const, CONSTS)
            eng.wait_ge(s_step, 4)
            nc.tensor.matmul(ps_a[0:1, 0:1], ext[:, 4:5], onescol[:, :], start=True, stop=True).then_inc(s_flagps, 1)

            def one_hot_turn(s, k):
                eng.wait_ge(L[0]["oh"], after(s))
                eng.wait_ge(L[0]["oht"], after(s - 1))
                for t in range(T):
                    last = nc.tensor.transpose(oht_ps[:, t, :], oh_b[:, k % 2, t, :], identb[:, :])
                last.then_inc(L[0]["oht_ps"], 1)

            def keys(n, s, k):
                eng.wait_ge(L[n]["keyf"], after(s))
                eng.wait_ge(L[n]["key_free"], after(s - 1))
                for t in range(T):
                    last = nc.tensor.transpose((key_ps0 if n == 0 else key_ps1)[:, t, :],
                                               keyf[:, k % 2, t:t + 1].to_broadcast([P, P]), ident[:, :])
                last.then_inc(L[n]["key_ps"], 1)

            def pick(s, k, i):
                eng.wait_ge(L[0]["oht"], after(s))
                eng.wait_ge(s_xwin[k % SLOTS], uses(i, k) * 16 + 16)
                eng.wait_ge(L[0]["msg"], after(s - 1))
                for t in range(T):
                    for m in range(NSPLIT):
                        last = nc.tensor.matmul(x_ps[:, t, :], oht[:, k % 2, t, :],
                                                xwin[:, k % SLOTS, m * D:(m + 1) * D],
                                                start=(m == 0), stop=(m == NSPLIT - 1))
                last.then_inc(L[0]["x_ps"], 1)

            def combine(n, s, k):
                eng.wait_ge(L[n]["msg"], after(s))
                eng.wait_ge(L[n]["same"], after(s))
                eng.wait_ge(L[n]["comb"], after(s - 1))
                for t in range(T):
                    last = nc.tensor.matmul((comb_ps0 if n == 0 else comb_ps1)[:, t, :],
                                            same[:, k % SLOTS, t, :], msg[:, k % 2, t, :], start=True, stop=True)
                last.then_inc(L[n]["comb_ps"], 1)

            def hidden(s, k, i):
                b = k // CHUNK % 2
                if k % CHUNK == 0:
                    eng.wait_ge(s_hs[b], (i + k // U) * (16 * NSPLIT) + 16 * NSPLIT)
                for c in range(2):
                    eng.wait_ge(L[1][f"ht{c}"], after(s - 1))
                    nc.tensor.matmul(ps_h[:, c, :], w1k[:, c * P:(c + 1) * P],
                                     hs[:, b, k % CHUNK * SB:(k % CHUNK + 1) * SB], start=True, stop=True)\
                        .then_inc(L[1][f"hps{c}"], 1)

            def weights(s, k):
                for c in range(2):
                    eng.wait_ge(L[1][f"ht{c}"], after(s))
                eng.wait_ge(L[1]["pv"], after(s - 2))
                for t in range(T):
                    at = 2 * (k % 2) + t // 2
                    for c in range(2):
                        last = nc.tensor.matmul(ps_w[:, at, t % 2 * HID:(t % 2 + 1) * HID],
                                                hT[:, k % 2, c, t * P:(t + 1) * P], w2s[:, c, :],
                                                start=(c == 0), stop=(c == 1))
                last.then_inc(L[1]["w_ps"], 1)

            def window_sum(s, k):
                eng.wait_ge(L[1]["msg"], after(s))
                eng.wait_ge(L[1]["oh"], after(s))
                eng.wait_ge(L[1]["added"], after(s - 2))
                for t in range(T):
                    last = nc.tensor.matmul(ps_acc[k % 2][t * D:(t + 1) * D, 0:WIN], msg[:, k % 2, t, :],
                                            oh[:, k % 2, t, :], start=True, stop=True)
                last.then_inc(L[1]["acc"], 1)

            def program(fast):
                for name in ("oht_ps", "key_ps", "x_ps", "comb_ps"):
                    eng.sem_inc(L[0][name], PRIME)
                for name in ("hps0", "hps1", "w_ps", "acc", "key_ps", "comb_ps"):
                    eng.sem_inc(L[1][name], PRIME)
                for k in range(2):
                    if fast:
                        one_hot_turn(k, k)
                    keys(0, k, k)
                if fast:
                    pick(0, 0, 0)

                def step0(s, k, i, more):
                    if more(2):
                        keys(0, s + 2, k + 2)
                    if fast and more(1):
                        pick(s + 1, k + 1, i)
                    combine(0, s, k)
                    if fast and more(2):
                        one_hot_turn(s + 2, k + 2)
                sweep(eng, step0)
                eng.wait_ge(s_w1k, 1)
                eng.wait_ge(s_w2, 1)
                eng.wait_ge(s_normed, PARTS)
                hidden(0, 0, 0)
                hidden(1, 1, 0)
                weights(0, 0)

                def step1(s, k, i, more):
                    if more(2):
                        hidden(s + 2, k + 2, i)
                    if more(1):
                        weights(s + 1, k + 1)
                    if not fast:
                        keys(1, s, k)
                    if not isinstance(s, int) or s >= 2:
                        target_sum(s - 2, k - 2)

                def target_sum(s, k):
                    if fast:
                        window_sum(s, k)
                    else:
                        combine(1, s, k)
                sweep(eng, step1, head=1)
                for d in (2, 1):
                    target_sum(NSB - d, U - d)
                if fast:
                    eng.wait_ge(L[1]["added"], after(NSB - 1))
                    eng.wait_ge(L[1]["pv"], after(NSB - 1))
                    acc_v = big[:, 0:NP].rearrange("f (p j) -> f j p", j=NJ)
                    for j in range(NJ):
                        if j % PJ == 0 and j >= 4 * PJ:
                            eng.wait_ge(s_turned_read, j // PJ - 3)
                        last = nc.tensor.matmul(ps_w[:, j // PJ % 4, j % PJ * D:(j % PJ + 1) * D],
                                                acc_v[:, j, :], stack[:, :], start=True, stop=True)
                        if j % PJ == PJ - 1:
                            last.then_inc(s_turned, 1)
            both(eng, program)

        @block.vector
        def _(eng):
            V = nc.vector
            x_rows = [v.rearrange("p (r f) -> p r f", f=D) for v in (x_f, x_r)]
            for h in range(XPARTS + 1):
                if h < XPARTS:
                    rows = slice(h * XR, (h + 1) * XR)
                    eng.wait_ge(s_xa, h + 1)
                    V.tensor_tensor(x_rows[1][:, rows], x_rows[0][:, rows], x_b[:, 0, rows], ALU.subtract)\
                        .then_inc(s_xr, 1)
                if h > 0:
                    rows = slice((h - 1) * XR, h * XR)
                    eng.wait_ge(s_xb, h)
                    V.tensor_tensor(x_b[:, 2, rows], x_rows[1][:, rows], x_b[:, 1, rows], ALU.subtract)\
                        .then_inc(s_xc, 1)

            eng.wait_ge(s_edges, 48)
            rel_v = rel[:, :].rearrange("p (s t) -> p s t", t=T)
            V.tensor_tensor(rel_v, dst_i[:, :].rearrange("p (s t) -> p s t", t=T),
                            spread(first_i[:, :], 2, T), ALU.subtract).then_inc(s_step, 1)
            eng.wait_ge(s_step, 1)
            V.tensor_scalar(nrel[:, :], rel[:, :], -1.0, None, ALU.mult).then_inc(s_nrel, 1)
            V.tensor_reduce(ext[:, 0:1], rel[:, :], AX_X, ALU.max).then_inc(s_step, 1)
            V.tensor_reduce(ext[:, 1:2], rel[:, :], AX_X, ALU.min).then_inc(s_step, 1)
            eng.wait_ge(s_step, 3)
            V.tensor_scalar(ext[:, 2:3], ext[:, 0:1], WIN - 0.5, None, ALU.is_gt).then_inc(s_ext, 1)
            V.tensor_scalar(ext[:, 3:4], ext[:, 1:2], -0.5, None, ALU.is_lt).then_inc(s_ext, 1)
            eng.wait_ge(s_ext, 2)
            V.tensor_tensor(ext[:, 4:5], ext[:, 2:3], ext[:, 3:4], ALU.add).then_inc(s_step, 1)
            eng.wait_ge(s_flagps, 1)
            V.tensor_scalar(flag_i[:, :], ps_a[0:1, 0:1], 0.5, None, ALU.is_gt).then_inc(s_flag, 1)

            eng.wait_ge(s_wload, 16 * 10)
            eng.wait_ge(s_const, CONSTS)
            w = lambda j: w1s[:, j, :]
            chain = [0]

            def link(ins):
                chain[0] += 1
                ins.then_inc(s_link, 1)
                eng.wait_ge(s_link, chain[0])
            link(V.tensor_copy(w1p[:, 0, :], w(0)))
            link(V.tensor_tensor(w(1), w(0), w1p[:, 0, :], ALU.subtract))
            link(V.tensor_copy(w1p[:, 1, :], w(1)))
            link(V.tensor_tensor(w(2), w(1), w1p[:, 1, :], ALU.subtract))
            link(V.tensor_copy(w1p[:, 2, :], w(2)))
            link(V.tensor_scalar(w(3), w1p[:, 0, :], w1m[:, 0:1], None, ALU.mult))
            link(V.scalar_tensor_tensor(w(4), w1p[:, 1, :], w1m[:, 1:2], w(3), ALU.mult, ALU.add))
            V.scalar_tensor_tensor(w1k[:, :], w1p[:, 2, :], w1m[:, 2:3], w(4), ALU.mult, ALU.add)\
                .then_inc(s_w1k, 1)
            scale = (1.0 / HID ** 0.5) * (1.0 / 128.0) ** 0.5 / (E / N) ** 0.5
            link(V.tensor_scalar(w2s[:, :, :], w2s[:, :, :], scale, None, ALU.mult))
            path1 = w2s[:, :, :].rearrange("p h (u c w) -> p (h u) c w", c=4, w=MUL)[:, :, 1, :]
            V.tensor_scalar(path1, path1, 1.0 / 3.0 ** 0.5, None, ALU.mult).then_inc(s_w2, 1)

            def split(k, i):
                if k == 2:
                    eng.wait_ge(s_esa, i + 1)
                    V.tensor_tensor(es_r, es_f, es_b[0][:, :], ALU.subtract).then_inc(s_esr, 1)
                if k == 4:
                    eng.wait_ge(s_esb, i + 1)
                    V.tensor_tensor(es_b[2][:, :], es_r, es_b[1][:, :], ALU.subtract).then_inc(s_esc, 1)

            def key_cast(n, s, k, ids):
                eng.wait_ge(L[n]["sidx"], after(s - 2))
                V.tensor_copy(keyf[:, k % 2, :], ids[:, bass.ds(s * T, T)]).then_inc(L[n]["keyf"], 1)

            def one_hot(s, k):
                eng.wait_ge(L[0]["oht_ps"], after(s - 2))
                V.tensor_tensor(oh_b[:, k % 2, :, :], spread(iota_ps, 1, T),
                                spread(rel[:, bass.ds(s * T, T)], 2, WIN), ALU.is_equal)\
                    .then_inc(L[0]["oh"], 1)

            def dedupe(n, s, k):
                b = k % 2
                key_ps = key_ps0 if n == 0 else key_ps1
                eng.wait_ge(L[n]["keyf"], after(s))
                eng.wait_ge(L[n]["key_ps"], after(s))
                eng.wait_ge(L[n]["comb"], after(s - SLOTS))
                V.tensor_tensor(same[:, k % SLOTS, :, :], key_ps, spread(keyf[:, b, :], 2, P), ALU.is_equal)\
                    .then_inc(L[n]["same"], 1)
                for t in range(T):
                    last = V.scalar_tensor_tensor(junk[:, t, :], key_ps[:, t, :], keyf[:, b, t:t + 1], tri[:, :],
                                                  ALU.is_equal, ALU.mult, accum_out=dup[:, b, 0, t:t + 1])
                last.then_inc(L[n]["key_free"], 1)
                V.tensor_scalar(dup[:, b, 1, :], keyf[:, b, :], -1.0, trash[:, :], ALU.mult, ALU.add)\
                    .then_inc(L[n]["scaled"], 1)
                eng.wait_ge(L[n]["key_free"], after(s))
                eng.wait_ge(L[n]["scaled"], after(s * 2))
                V.scalar_tensor_tensor(dup[:, b, 2, :], dup[:, b, 0, :], 0.5, dup[:, b, 1, :],
                                       ALU.is_gt, ALU.mult).then_inc(L[n]["scaled"], 1)
                eng.wait_ge(L[n]["scaled"], after(s * 2 + 1))
                eng.wait_ge(L[n]["retired"], s * T + T)
                V.tensor_tensor(sidx[:, k % RING, :], dup[:, b, 2, :], keyf[:, b, :], ALU.add)\
                    .then_inc(L[n]["sidx"], 1)

            def message(s, k, i, fast):
                eng.wait_ge(L[0]["comb"], after(s - 2))
                if fast:
                    eng.wait_ge(L[0]["x_ps"], after(s))
                    rows = x_ps
                else:
                    eng.wait_ge(s_gat[0][k % SLOTS], uses(i, k) * 16 * T + 16 * T)
                    rows = gat[:, k % SLOTS, :, :]
                V.tensor_tensor(msg[:, k % 2, :, :], rows, spread(wgt[:, bass.ds(s * T, T)], 2, D), ALU.mult)\
                    .then_inc(L[0]["msg"], 1)

            def pair_sh(s):
                return sh_sb[:, bass.ds(s * (4 * T), 8 * T)].rearrange("p (t c) -> p t c", c=4)[:, :, 1:4]

            def dots_products(s, k, i):
                q = k % SLOTS
                for d in range(2):
                    eng.wait_ge(s_gat[1][q + d], uses(i, k) * 16 * T + 16 * T)
                eng.wait_ge(L[1]["dot"], after(s - 1))
                V.tensor_tensor(vv[:, :, :, :],
                                gat[:, q:q + 2, :, :].rearrange("p q t (u c) -> p (q t) u c", c=4)[:, :, :, 1:4],
                                spread(pair_sh(s), 2, MUL), ALU.mult).then_inc(L[1]["pre"], 2)

            def dots(s, k):
                eng.wait_ge(L[1]["pre"], after(s + 1))
                eng.wait_ge(L[1]["pv"], after(s - 1))
                V.tensor_reduce(coef[:, :, :, 1].rearrange("p b g -> p (b g)"),
                                vv[:, :, :, :].rearrange("p t u i -> p (t u) i"),
                                AX_X, ALU.add).then_inc(L[1]["dot"], 2)

            def weights_at(k):
                return ps_w[:, 2 * (k % 2):2 * (k % 2) + 2, :].rearrange("p b (g c w) -> p (b g) c w", c=4, w=MUL)

            def vector_products(s, k):
                eng.wait_ge(L[1]["w_ps"], after(s))
                eng.wait_ge(L[1]["coef"], after(s))
                eng.wait_ge(L[1]["rv"], after(s - 1))
                V.tensor_tensor(prod[:, :, 3:6, :], spread(weights_at(k)[:, :, 3, :], 2, 3),
                                spread(coef[:, k % 2, :, 3:6], 3, MUL), ALU.mult)

            def scalar_products(s, k):
                eng.wait_ge(L[1]["dot"], after(s))
                V.tensor_tensor(prod[:, :, 0:3, :], weights_at(k)[:, :, 0:3, :],
                                spread(coef[:, k % 2, :, 0:3], 3, MUL), ALU.mult).then_inc(L[1]["pv"], 1)

            def sum_products(s, k):
                eng.wait_ge(L[1]["pv"], after(s))
                eng.wait_ge(L[1]["msg"], after(s - 2))
                V.tensor_reduce(red[:, k % 2 * T:(k % 2 + 1) * T, 0:6, :].rearrange("p t c w -> p t (c w)"),
                                prod[:, :, :, :].rearrange("p (t u) c w -> p t (c w) u", u=MUL), AX_X, ALU.add)\
                    .then_inc(L[1]["rv"], 1)

            def cross(s):
                eng.wait_ge(L[1]["rv"], after(s + 1))
                V.tensor_tensor(red[:, :, 1 + CROSS::CROSS, :], spread(red[:, :, 0, :], 2, 3),
                                spread(pair_sh(s), 3, MUL), ALU.mult).then_inc(L[1]["cross"], 2)

            def messages(s, fast):
                eng.wait_ge(L[1]["cross"], after(s + 1))
                eng.wait_ge(L[1]["acc" if fast else "comb_ps"], after(s - 1))
                V.tensor_tensor(msg[:, :, :, :].rearrange("p b t (c w) -> p (b t) c w", w=MUL), red[:, :, 2:6, :],
                                red[:, :, 1::CROSS, :], ALU.add).then_inc(L[1]["msg"], 2)

            def window_at(s):
                return eng.value_load(first_i[0:1, bass.ds(s, 1)], min_val=0, max_val=N - 1)

            def add_window(s, k, base):
                eng.wait_ge(L[1]["acc"], after(s))
                eng.wait_ge(L[1]["added"], after(s - 1))
                V.tensor_tensor(big[:, bass.ds(base, WIN)], ps_acc[k % 2][:, 0:WIN], big[:, bass.ds(base, WIN)],
                                ALU.add).then_inc(L[1]["added"], 1)

            def norm(n, fast):
                done = n * PARTS
                rows = lambda v: v.rearrange("p (j f) -> p j f", f=D)
                zv = lambda c: rows(work[:, part(c)])
                st = lambda k, c: stat[:, k, c * PJ:(c + 1) * PJ]
                turned = n == 1 and fast
                for c in range(PARTS + 3):
                    if c >= 3:
                        eng.wait_ge(s_std, done + c - 2)
                        V.reciprocal(st(3, c - 3), st(2, c - 3)).then_inc(s_recip, 1)
                    if c < PARTS and turned:
                        eng.wait_ge(s_turned, c + 1)
                        add_nodes(c, rows(ps_w[:, c % 4, 0:PJ * D])).then_inc(s_turned_read, 1)
                    if c < PARTS and not turned:
                        eng.wait_ge(s_tab[c], 16 * T * (n + 1))
                        V.tensor_tensor(work[:, part(c)], big[:, part(c)], big[:, part(c, 1)], ALU.add)\
                            .then_inc(s_two, 1)
                    if 1 <= c <= PARTS:
                        eng.wait_ge(s_turned_read if turned else s_joined, c if turned else done + c)
                        V.tensor_reduce(st(0, c - 1), zv(c - 1), AX_X, ALU.add).then_inc(s_rowsum, 1)
                    if c >= 3:
                        eng.wait_ge(s_recip, done + c - 2)
                        scale(n, c - 3, zv(c - 3), st(3, c - 3))
                    if c < PARTS and not turned:
                        eng.wait_ge(s_two, done + c + 1)
                        eng.wait_ge(s_other, done + c + 1)
                        if n == 0:
                            V.tensor_tensor(work[:, part(c)], work[:, part(c)], big[:, part(c, 2)], ALU.add)\
                                .then_inc(s_joined, 1)
                        else:
                            link(V.tensor_tensor(big[:, part(c, 1)], work[:, part(c)], big[:, part(c, 2)], ALU.add))
                            add_nodes(c, rows(big[:, part(c, 1)])).then_inc(s_joined, 1)
                    if 1 <= c <= PARTS:
                        eng.wait_ge(s_rowsum, done + c)
                        V.tensor_scalar(stat[:, 0, (c - 1) * PJ:c * PJ], st(0, c - 1), -1.0 / D, None, ALU.mult)\
                            .then_inc(s_mean, 1)
                    if 2 <= c <= PARTS + 1:
                        eng.wait_ge(s_squared, done + c - 1)
                        V.tensor_reduce(st(1, c - 2), rows(squares(c - 2)), AX_X, ALU.add).then_inc(s_summed, 1)
                    if 1 <= c <= PARTS:
                        eng.wait_ge(s_mean, done + c)
                        V.tensor_tensor(zv(c - 1), zv(c - 1), spread(st(0, c - 1), 2, D), ALU.add)\
                            .then_inc(s_centred, 1)

            def scale(n, c, zv, factor):
                if n == 1:
                    V.tensor_tensor(zv, zv, spread(factor, 2, D), ALU.mult).then_inc(s_normed, 1)
                    return
                dv = x1[:, part(c)].rearrange("p (g c) -> p g c", c=4)
                V.tensor_tensor(dv[:, :, 0].rearrange("p (j u) -> p j u", u=MUL), zv[:, :, 0:MUL],
                                spread(factor, 2, MUL), ALU.mult)
                V.tensor_tensor(dv[:, :, 1:4].rearrange("p (j u) i -> p j u i", u=MUL),
                                zv[:, :, MUL:D].rearrange("p j (u i) -> p j u i", i=3),
                                spread(spread(factor, 2, MUL), 3, 3), ALU.mult).then_inc(s_normed, 1)

            def program(fast):
                saved = chain[0]
                for name in ("keyf", "oh", "same", "key_free", "scaled", "sidx", "msg"):
                    eng.sem_inc(L[0][name], PRIME)
                for name in ("keyf", "same", "key_free", "scaled", "sidx", "msg", "pre", "dot",
                             "pv", "rv", "cross", "added"):
                    eng.sem_inc(L[1][name], PRIME)
                eng.wait_ge(s_iotab, 1)
                eng.wait_ge(s_w, 16)
                def prepare(s, k):
                    key_cast(0, s, k, src_i)
                    if fast:
                        one_hot(s, k)

                for k in range(2):
                    prepare(k, k)
                    dedupe(0, k, k)
                message(0, 0, 0, fast)
                prepare(2, 2)

                def step0(s, k, i, more):
                    if more(3):
                        prepare(s + 3, k + 3)
                    if more(1):
                        message(s + 1, k + 1, i, fast)
                    if more(2):
                        dedupe(0, s + 2, k + 2)
                    split(k, i)
                sweep(eng, step0)
                norm(0, fast)
                if fast:
                    eng.wait_ge(s_cleared, PARTS + 1)
                eng.wait_ge(s_sh, 16 * U)

                dots_products(0, 0, 0)
                dots(0, 0)

                def step1(s, k, i, more):
                    before = s if isinstance(s, int) else NSB
                    pair_in = k % 2 == 0 and before >= 2
                    if not fast:
                        key_cast(1, s, k, dst_i)
                        dedupe(1, s, k)
                    vector_products(s, k)
                    adding = fast and k % 2 == 0 and before >= 4
                    if adding:
                        base = window_at(s - 4)
                    if pair_in:
                        cross(s - 2)
                    scalar_products(s, k)
                    if pair_in:
                        messages(s - 2, fast)
                    if k % 2 and more(1):
                        dots_products(s + 1, k + 1, i)
                    if adding:
                        add_window(s - 4, k, base)
                    sum_products(s, k)
                    if adding:
                        add_window(s - 3, k + 1, window_at(s - 3))
                    if k % 2 and more(1):
                        dots(s + 1, k + 1)
                sweep(eng, step1, head=1)
                cross(NSB - 2)
                messages(NSB - 2, fast)
                if fast:
                    for d in range(4, 0, -1):
                        add_window(NSB - d, U - d, window_at(NSB - d))
                norm(1, fast)
                chain[0] = saved

            def add_nodes(c, sums):
                xv = x1[:, part(c)].rearrange("p (j u c) -> p j u c", u=MUL, c=4)
                wv = work[:, part(c)].rearrange("p (j f) -> p j f", f=D)
                V.tensor_tensor(wv[:, :, 0:MUL], xv[:, :, :, 0], sums[:, :, 0:MUL], ALU.add)
                return V.tensor_tensor(wv[:, :, MUL:D].rearrange("p j (w i) -> p j w i", i=3), xv[:, :, :, 1:4],
                                       sums[:, :, MUL:D].rearrange("p j (i w) -> p j w i", i=3), ALU.add)
            both(eng, program)




def kernel(x, src, dst, edge_attr_4, edge_attr_8, edge_weight, L1_gnn_fc_w1, L1_gnn_fc_w2):
    import numpy as np
    import concourse.bacc as bacc
    from concourse.bass_utils import run_bass_kernel_spmd

    def edges(a, how="constant"):
        a = np.pad(np.asarray(a), [(0, EP - E)] + [(0, 0)] * (a.ndim - 1), mode=how)
        return a.reshape(NSB, P, T, -1)

    def on_partitions(a):
        return np.ascontiguousarray(a.transpose(1, 0, 2, 3).reshape(P, -1))

    targets = edges(dst, "edge")
    w2 = np.asarray(L1_gnn_fc_w2).reshape(HID, 4, MUL, MUL)
    w2 = w2[:, [2, 1, 0, 3]].transpose(0, 2, 1, 3).reshape(HID, -1)
    arrays = {
        "x": np.pad(np.asarray(x), [(0, ROWS - N), (0, 0)]),
        "src": on_partitions(edges(src)),
        "dst": on_partitions(targets),
        "first": np.ascontiguousarray(np.broadcast_to(targets[:, 0, 0, 0], (P, NSB))),
        "weight": on_partitions(edges(edge_weight)),
        "sh": on_partitions(edges(edge_attr_4)),
        "es": np.ascontiguousarray(edges(edge_attr_8).transpose(3, 0, 2, 1).reshape(BASIS, EP)),
        "w1": np.ascontiguousarray(L1_gnn_fc_w1),
        "w2": np.ascontiguousarray(w2),
    }
    nc = bacc.Bacc("TRN2", target_bir_lowering=False, num_devices=1)
    args = [nc.dram_tensor(name, a.shape, mybir.dt.from_np(a.dtype), kind="ExternalInput").ap()
            for name, a in arrays.items()]
    out = nc.dram_tensor("out", (NP, D), F32, kind="ExternalOutput").ap()
    gnn_kernel(nc, *args, out)
    r = run_bass_kernel_spmd(nc, [arrays], core_ids=[0])
    return r.results[0]["out"][0:N]
```
